# Optimizing a Trainium2 kernel written in Bass

```python
import numpy as np
import jax
import jax.numpy as jnp

def _softmax(x, axis=-1):
    return jax.nn.softmax(x, axis=axis)

def _gelu(x):
    return jax.nn.gelu(x, approximate=True)

def _silu(x):
    return jax.nn.silu(x)

def _sigmoid(x):
    return jax.nn.sigmoid(x)

def _layernorm(x, axis=-1, eps=1e-05):
    m = jnp.mean(x, axis=axis, keepdims=True)
    v = jnp.var(x, axis=axis, keepdims=True)
    return (x - m) / jnp.sqrt(v + eps)

def _scatter_add(tgt, idx, src, axis=0):
    return tgt.at[idx].add(src)

def _segment_sum(src, seg, n):
    return jax.ops.segment_sum(src, seg, n)
kernel_name = 'mk_adj_ffn_d1_adj_r2_ab10ce'

def setup_inputs(seed: int=0):
    np.random.seed(seed)
    _w = jnp.asarray

    def _rec_inputs():
        import jax
        import jax.numpy as jnp
        _gk = jax.random.key(seed)
        x = -0.0002144 + 1 * jax.random.normal(jax.random.fold_in(_gk, 1), (128, 64, 128), jnp.float32)
        _w = (1.0 + jnp.arange(64, dtype=jnp.float32)) ** (-0.5)
        _w = _w / _w.mean()
        _pij = jnp.clip(0.0625 * _w[:, None] * _w[None, :], 0.0, 1.0)
        _a = jax.random.uniform(jax.random.fold_in(_gk, 2), (128, 64, 64)) < _pij
        adj = _a.astype(jnp.int32)
        return (x, adj)
    x, adj = _rec_inputs()

    def _L0_gnn_setup():
        import jax, jax.numpy as jnp
        import numpy as np
        B, N, D, T = (256, 50, 128, 64)
        NEG = -9000000000000000.0
        LRELU_SLOPE = 0.2
        key = jax.random.key(seed)
        k0, k1, k2, k3, k4 = jax.random.split(key, 5)
        hidden = jax.random.normal(k0, (B, N, D), dtype=jnp.float32)
        adj = jax.random.randint(k1, (B, N, N), 0, 6, dtype=jnp.int32)
        A_interval = jax.random.uniform(k2, (B, N, N), dtype=jnp.float32)
        stdv = 1.0 / np.sqrt(D)
        a_rel = jax.random.uniform(k3, (5, D), dtype=jnp.float32, minval=-stdv, maxval=stdv)
        t_rel = jax.random.uniform(k4, (5, T), dtype=jnp.float32, minval=-stdv, maxval=stdv)
        time_w = jnp.asarray(1.0 / 10.0 ** np.linspace(0, 9, T, dtype=np.float32))
        return {'hidden': hidden, 'adj': adj, 'A_interval': A_interval, 'a_rel': a_rel, 't_rel': t_rel, 'time_w': time_w}
    _L0_gnn_all = _L0_gnn_setup()
    _L0_gnn_in = {k: v for k, v in _L0_gnn_all.items() if k in ('a_rel', 't_rel', 'time_w')}
    del _L0_gnn_all

    def _L0_ffn_setup():
        import jax, jax.numpy as jnp
        import numpy as np
        B, S, D, F, E, K = (8, 1024, 128, 512, 8, 2)
        key = jax.random.key(seed)
        ks = jax.random.split(key, 10)
        s = 0.02
        return {'x': jax.random.normal(ks[0], (B, S, D), dtype=jnp.float32), 'Wr': jax.random.normal(ks[1], (D, E), dtype=jnp.float32) * s, 'W1s': jax.random.normal(ks[2], (D, F), dtype=jnp.float32) * s, 'b1s': jnp.zeros((F,), dtype=jnp.float32), 'W2s': jax.random.normal(ks[3], (F, D), dtype=jnp.float32) * s, 'b2s': jnp.zeros((D,), dtype=jnp.float32), 'W1p': jax.random.normal(ks[4], (E, D, F), dtype=jnp.float32) * s, 'b1p': jnp.zeros((E, F), dtype=jnp.float32), 'W2p': jax.random.normal(ks[5], (E, F, D), dtype=jnp.float32) * s, 'b2p': jnp.zeros((E, D), dtype=jnp.float32)}
    _L0_ffn_all = _L0_ffn_setup()
    _L0_ffn_in = {k: v for k, v in _L0_ffn_all.items() if k in ('Wr', 'W1s', 'b1s', 'W2s', 'b2s', 'W1p', 'b1p', 'W2p', 'b2p')}
    del _L0_ffn_all
    return {'x': x, 'adj': adj, 'L0_gnn_a_rel': _L0_gnn_in['a_rel'], 'L0_gnn_t_rel': _L0_gnn_in['t_rel'], 'L0_gnn_time_w': _L0_gnn_in['time_w'], 'L0_ffn_Wr': _L0_ffn_in['Wr'], 'L0_ffn_W1s': _L0_ffn_in['W1s'], 'L0_ffn_b1s': _L0_ffn_in['b1s'], 'L0_ffn_W2s': _L0_ffn_in['W2s'], 'L0_ffn_b2s': _L0_ffn_in['b2s'], 'L0_ffn_W1p': _L0_ffn_in['W1p'], 'L0_ffn_b1p': _L0_ffn_in['b1p'], 'L0_ffn_W2p': _L0_ffn_in['W2p'], 'L0_ffn_b2p': _L0_ffn_in['b2p']}

def reference(x, adj, L0_gnn_a_rel, L0_gnn_t_rel, L0_gnn_time_w, L0_ffn_Wr, L0_ffn_W1s, L0_ffn_b1s, L0_ffn_W2s, L0_ffn_b2s, L0_ffn_W1p, L0_ffn_b1p, L0_ffn_W2p, L0_ffn_b2p):
    import jax
    import jax.numpy as jnp

    def _L0_gnn_ref(hidden, adj, A_interval, a_rel, t_rel, time_w):
        import jax, jax.numpy as jnp
        import numpy as np
        B, N, D, T = (256, 50, 128, 64)
        NEG = -9000000000000000.0
        LRELU_SLOPE = 0.2
        e_struct = jnp.einsum('bid,bjd,rd->bijr', hidden, hidden, a_rel)
        tenc = jax.lax.stop_gradient(jnp.cos(A_interval[..., None] * time_w))
        e_time = jnp.einsum('bijt,rt->bijr', tenc, t_rel)
        e = jax.nn.leaky_relu(e_struct + e_time, negative_slope=LRELU_SLOPE)
        idx = jnp.clip(adj - 1, 0, 4)[..., None]
        sel = jnp.take_along_axis(e, idx, axis=-1)[..., 0]
        alpha = jnp.where((adj >= 1) & (adj <= 5), sel, NEG)
        alpha = jax.nn.softmax(alpha, axis=-1)
        return jnp.einsum('bij,bjd->bid', alpha, hidden)

    def _L0_ffn_ref(x, Wr, W1s, b1s, W2s, b2s, W1p, b1p, W2p, b2p):
        import jax, jax.numpy as jnp
        import numpy as np
        B, S, D, F, E, K = (8, 1024, 128, 512, 8, 2)
        gelu = lambda t: jax.nn.gelu(t, approximate=False)
        shared = gelu(x @ W1s + b1s) @ W2s + b2s
        rw = jax.nn.softmax(x @ Wr, axis=-1)
        topw, topi = jax.lax.top_k(rw, K)
        topw = topw / jnp.sum(topw, axis=-1, keepdims=True)
        mask = jnp.sum(jax.nn.one_hot(topi, E, dtype=topw.dtype) * topw[..., None], axis=-2)
        h = gelu(jnp.einsum('bsd,edf->bsef', x, W1p) + b1p)
        priv = jnp.einsum('bsef,efd->bsed', h, W2p) + b2p
        routed = jnp.einsum('bsed,bse->bsd', priv, mask)
        return shared + routed
    x = x + _L0_gnn_ref(_layernorm(x, axis=-1), adj, adj, L0_gnn_a_rel, L0_gnn_t_rel, L0_gnn_time_w)
    x = x + _L0_ffn_ref(_layernorm(x, axis=-1), L0_ffn_Wr, L0_ffn_W1s, L0_ffn_b1s, L0_ffn_W2s, L0_ffn_b2s, L0_ffn_W1p, L0_ffn_b1p, L0_ffn_W2p, L0_ffn_b2p)
    return x

_drawn_inputs = setup_inputs


def setup_inputs(seed=0):
    import zlib

    import numpy as np

    out = dict(_drawn_inputs(seed))
    spreads = {'L0_ffn_b1s': (0.0, 0.402),
     'L0_ffn_b2s': (0.0, 0.1),
     'L0_ffn_b1p': (0.0, 0.549),
     'L0_ffn_b2p': (0.0, 0.1)}
    factors = {'L0_gnn_time_w': 8.0}
    for name, (base, spread) in spreads.items():
        noise = np.random.default_rng([zlib.crc32(name.encode()), seed]).standard_normal(out[name].shape)
        drawn = base * np.exp(spread * noise) if base else spread * noise
        out[name] = jnp.asarray(drawn.astype(out[name].dtype))
    for name, factor in factors.items():
        out[name] = (out[name] * factor).astype(out[name].dtype)
    return out
```

```python
from contextlib import ExitStack

import concourse.bass as bass
from concourse import mybir

F32 = mybir.dt.float32
F16 = mybir.dt.float16
BF16 = mybir.dt.bfloat16
I32 = mybir.dt.int32
U32 = mybir.dt.uint32
ALU = mybir.AluOpType
ACT = mybir.ActivationFunctionType
AX = mybir.AxisListType

P = 128
GRAPHS, NODES, D = 128, 64, 128
TOKENS = GRAPHS * NODES
RELATIONS = 5
TIMES = 64
E = 8
F = 512
FC = F // P
TOP = 2
TPG = 4
GROUP = TPG * P
GROUPS = TOKENS // GROUP
TILES = TOKENS // P
GN = TPG * NODES
SB = (RELATIONS + 1) // 2
RB = 256
RH = RB // P
REGION = TOKENS + RB
RTILES = TOP * TOKENS // RB + E
ROWS = E * REGION + E * RB
RW = D + 2
YROWS = TOP * TOKENS + 2 * E * RB
EPS = 1e-5
NEG = -9000000000000000.0
SLOPE = 0.2
XS = 2.0 ** 6
WS = 2.0 ** 8
UNSCALE = 1.0 / (XS * WS)
TWO_PI = 6.283185307179586
PI_HI = 6.28125
PI_MID = 0.0019350051879882812
PI_LO = 3.0199159819597e-07
HALF_PI = TWO_PI / 4
MAGIC = 12582912.0

C_IDENT, C_TRI, C_IOTA, C_REGION, C_PART, C_REL, C_TILE = 0, P, 2 * P, 2 * P + E, 2 * P + 2 * E, 2 * P + 2 * E + 3, 2 * P + 2 * E + 3 + RELATIONS
C_ALL = C_TILE + RTILES
K_PLACE, K_PAD, K_SPARE = 0, TPG * TOP, TPG * TOP + E * RH
K_ALL = K_SPARE + E * RH


def build(nc, x, adj, a_relT, t_relT, time_w, wr, w1, w2, b1T, b2, constants, places, out, rows_dram, results_dram):
    x_v = x.rearrange("(t p) d -> p t d", p=P)
    adj_v = adj.rearrange("(t p) n -> p t n", p=P)
    out_v = out.rearrange("(t p) d -> p t d", p=P)
    results_v = results_dram[0:TOP * TOKENS, :].rearrange("(k t p) d -> p k t d", p=P, k=TOP)

    with ExitStack() as ctx:
        def sb(name, shape, dt):
            return ctx.enter_context(nc.sbuf_tensor(name, shape, dt))

        def sem(name):
            return ctx.enter_context(nc.semaphore(name))

        cst = sb("cst", [P, C_ALL], F32)
        plc = sb("plc", [P, K_ALL], I32)
        ident = cst[:, C_IDENT:C_IDENT + P]
        arel = sb("arel", [P, RELATIONS], F32)
        wr_f = sb("wr_f", [P, E], F32)
        wr_h = sb("wr_h", [P, E], F16)
        wr_l = sb("wr_l", [P, E], F16)
        w1_f = sb("w1_f", [P, (E + 1) * F], F32)
        w1_h = sb("w1_h", [P, E + 1, FC, P], F16)
        w1_l = sb("w1_l", [P, E + 1, FC, P], F16)
        w2_f = sb("w2_f", [P, E + 1, FC, D], F32)
        b1_f = sb("b1_f", [P, (E + 1) * FC], F32)
        b2_f = sb("b2_f", [P, E + 1, D], F32)
        tri = sb("tri", [P, P], BF16)
        ones = sb("ones", [P, P], BF16)
        ones_f = sb("ones_f", [TIMES, P], F32)
        minus_half = sb("minus_half", [P, TPG], F32)
        tw = sb("tw", [TIMES, 1], F32)
        trel = sb("trel", [TIMES, RELATIONS], F32)
        ang = sb("ang", [TIMES, 4, RELATIONS], F32)
        tsum = sb("tsum", [P, RELATIONS], F32)
        tparts = sb("tparts", [P, 3, RELATIONS], BF16)
        trest = sb("trest", [P, 2, RELATIONS], F32)
        trow = sb("trow", [P, 3, RELATIONS], F32)
        time_rows = sb("time_rows", [P, RELATIONS, GN], BF16)
        acc = sb("acc", [P, TILES, D], F32)
        xh = sb("xh", [P, TOKENS], F16)
        xl = sb("xl", [P, TOKENS], F16)
        gates = sb("gates", [P, TILES, TOP], F32)
        adj_sb = sb("adj_sb", [P, 2, TPG * NODES], I32)
        is_rel = sb("is_rel", [P, 2, RELATIONS, TPG * NODES], I32)
        st1 = sb("st1", [P, 2, TPG, 6], F32)
        mv1 = sb("mv1", [P, 2, TPG, 2], F32)
        ve1 = sb("ve1", [P, 2, TPG], F32)
        rstd1 = sb("rstd1", [P, 2, TPG], F32)
        st2 = sb("st2", [P, 2, TPG, 6], F32)
        mv2 = sb("mv2", [P, 2, TPG, 2], F32)
        ve2 = sb("ve2", [P, 2, TPG], F32)
        rstd2 = sb("rstd2", [P, 2, TPG], F32)
        xn = sb("xn", [P, 2, TPG, D], F32)
        xnT = sb("xnT", [P, 2, GROUP], F32)
        axT = sb("axT", [P, RELATIONS, GROUP], F32)
        sel = sb("sel", [P, 2, TPG, NODES], F32)
        lsel = sb("lsel", [P, 2, TPG, NODES], F32)
        nmax = sb("nmax", [P, 2, TPG], F32)
        prob = sb("prob", [P, 2, TPG, NODES], F32)
        psum_p = sb("psum_p", [P, 2, TPG], F32)
        rsum = sb("rsum", [P, 2, TPG], F32)
        diag = sb("diag", [P, 2, TPG, P], F32)
        rowbuf = sb("rowbuf", [P, 2, TPG, TOP, RW], F32)
        place = sb("place", [P, TPG, TOP], I32)
        logit = sb("logit", [P, TPG, E], F32)
        top8 = sb("top8", [P, TPG, E], F32)
        idx8 = sb("idx8", [P, TPG, E], U32)
        idxf = sb("idxf", [P, TPG, TOP], F32)
        onehot = sb("onehot", [P, 2, TPG, TOP, E], F32)
        chosen = sb("chosen", [P, 2, TPG, E], BF16)
        count_g = sb("count_g", [P, E], F32)
        count = sb("count", [P, 3, E], BF16)
        gap = sb("gap", [P, TPG], F32)
        egap = sb("egap", [P, 2, TPG], F32)
        e1 = sb("e1", [P, TPG], F32)
        slot = sb("slot", [P, TPG, E], F32)
        slot2 = sb("slot2", [P, TPG, TOP, E], F32)
        pos = sb("pos", [P, 2, TPG, TOP], I32)
        total = sb("total", [P, E], F32)
        total_i = sb("total_i", [P, E], I32)
        first_pad = sb("first_pad", [P, E], I32)
        n_i = sb("n_i", [P, E], I32)
        n_f = sb("n_f", [P, E], F32)
        cum = sb("cum", [P, 3, E], F32)
        past = sb("past", [1, RTILES, E], F32)
        past_n = sb("past_n", [1, RTILES, E], F32)
        tile_e = sb("tile_e", [1, RTILES], F32)
        tile_b = sb("tile_b", [1, RTILES], F32)
        tile_r = sb("tile_r", [1, RTILES], F32)
        etab = sb("etab", [1, RTILES], I32)
        rtab = sb("rtab", [1, RTILES], I32)
        padrows = sb("padrows", [P, E * RH, RW], F32)
        hid = axT[:, 0:FC, :]
        hid2 = sb("hid2", [P, FC, GROUP], F32)
        xt = sb("xt", [P, 2, RH, RW], F32)
        xth = sb("xth", [P, 2, RB], F16)
        xtl = sb("xtl", [P, 2, RB], F16)
        yt = xn[:, :, 0:RH, :]
        xid = sb("xid", [P, 2, RH], I32)
        yid = sb("yid", [P, 2, RH], I32)
        yb = w1_f[:, 0:2 * TOP * TPG * D].rearrange("p (c k t d) -> p c k t d", c=2, k=TOP, t=TPG)

        bank = ctx.enter_context(nc.psum_tensor("bank", [P, 8, 512], F32))

        xnT_ps, x2T_ps, prT_ps, att_ps = (bank[:, b, :] for b in (3, 4, 5, 6))
        router_ps = bank[:, 7, 0:TPG * E].rearrange("p (t e) -> p t e", e=E)
        rank_ps = bank[:, 7, 64:64 + TPG * E].rearrange("p (t e) -> p t e", e=E)
        total_ps = bank[:, 7, 128:128 + E]

        s_const = sem("s_const")
        s_weights = sem("s_weights")
        s_x = [sem("s_x_even"), sem("s_x_odd")]
        s_adj = [sem("s_adj0"), sem("s_adj1")]
        s_held = sem("s_held")
        s_setup = sem("s_setup")
        s_angle = sem("s_angle")
        s_cos = sem("s_cos")
        s_tprod = sem("s_tprod")
        s_tsum = sem("s_tsum")
        s_trow = sem("s_trow")
        s_time = sem("s_time")
        s_prep = sem("s_prep")
        s_w1h = sem("s_w1h")
        s_w1l = sem("s_w1l")
        s_bn1 = sem("s_bn1")
        s_mv1 = sem("s_mv1")
        s_ve1 = sem("s_ve1")
        s_rstd1 = sem("s_rstd1")
        s_xn = sem("s_xn")
        s_isrel = sem("s_isrel")
        s_xnT_ps = sem("s_xnT_ps")
        s_xnT = sem("s_xnT")
        s_axT = sem("s_axT")
        s_fill = sem("s_fill")
        s_scores = sem("s_scores")
        s_picked = sem("s_picked")
        s_lsel = sem("s_lsel")
        s_nmax = sem("s_nmax")
        s_prob = sem("s_prob")
        s_prT_ps = sem("s_prT_ps")
        s_diag = sem("s_diag")
        s_rsum = sem("s_rsum")
        s_att_ps = sem("s_att_ps")
        s_after = sem("s_after")
        s_bn2 = sem("s_bn2")
        s_mv2 = sem("s_mv2")
        s_ve2 = sem("s_ve2")
        s_rstd2 = sem("s_rstd2")
        s_xn2 = sem("s_xn2")
        s_x2T_ps = sem("s_x2T_ps")
        s_xh = sem("s_xh")
        s_xl = sem("s_xl")
        s_router = sem("s_router")
        s_logit = sem("s_logit")
        s_top8 = sem("s_top8")
        s_idx8 = sem("s_idx8")
        s_idxf = sem("s_idxf")
        s_onehot = sem("s_onehot")
        s_chosen = sem("s_chosen")
        s_count_g = sem("s_count_g")
        s_count = sem("s_count")
        s_gap = sem("s_gap")
        s_egap = sem("s_egap")
        s_e1 = sem("s_e1")
        s_gate0 = sem("s_gate0")
        s_gates = sem("s_gates")
        s_rank = sem("s_rank")
        s_slot = sem("s_slot")
        s_slot2 = sem("s_slot2")
        s_pos = sem("s_pos")
        s_placed = sem("s_placed")
        s_sent = [sem("s_sent0"), sem("s_sent1")]
        s_spare = sem("s_spare")
        s_padids = sem("s_padids")
        s_padded = sem("s_padded")
        s_total_ps = sem("s_total_ps")
        s_tab = sem("s_tab")
        s_table = sem("s_table")
        s_sh_up = sem("s_sh_up")
        s_sh_hid = sem("s_sh_hid")
        s_sh_down = sem("s_sh_down")
        s_sh_bias = sem("s_sh_bias")
        s_sh_acc = sem("s_sh_acc")
        s_xt = [sem("s_xt0"), sem("s_xt1")]
        s_xtT_ps = sem("s_xtT_ps")
        s_xth = sem("s_xth")
        s_xtl = sem("s_xtl")
        s_up = sem("s_up")
        s_hid = sem("s_hid")
        s_down = sem("s_down")
        s_xid = sem("s_xid")
        s_yt = sem("s_yt")
        s_ysent = [sem("s_ysent0"), sem("s_ysent1")]
        s_yb = [sem("s_yb0"), sem("s_yb1")]
        s_add0 = sem("s_add0")
        s_add = sem("s_add")
        s_out = sem("s_out")

        CONST_DMAS = 8
        block = ctx.enter_context(nc.Block())

        def pipeline(engine, body, n, before, after):
            for i in range(-before, 4):
                body(i // 2, i % 2, i)
            with engine.Fori(2, (n - 2) // 2) as k:
                body(k, 0, None)
                body(k, 1, None)
            for i in range(n - 2, n + after):
                body(i // 2, i % 2, i)

        def hold(engine, semaphore, value):
            engine.wait_ge(semaphore, value)
            engine.sem_inc(s_held, 1)

        def has(i, d, n):
            return i is None or 0 <= i + d < n

        @block.sync
        def _(sp):
            sp.dma_start(cst[:, :], constants).then_inc(s_const, 16)
            sp.dma_start(plc[:, :], places).then_inc(s_const, 16)
            sp.dma_start(arel[:, :], a_relT).then_inc(s_const, 16)
            sp.dma_start(tw[:, :], time_w).then_inc(s_const, 16)
            sp.dma_start(trel[:, :], t_relT).then_inc(s_const, 16)
            sp.dma_start(wr_f[:, :], wr).then_inc(s_const, 16)
            sp.dma_start(b1_f[:, :], b1T).then_inc(s_const, 16)
            sp.dma_start(b2_f[:, :, :].rearrange("p e d -> p (e d)"), b2).then_inc(s_const, 16)

            def load_group(k, c, i):
                g = 2 * k + c
                if i is None or i >= 2:
                    sp.wait_ge(s_x[c], 16 * k)
                    sp.wait_ge(s_adj[c], 16 * k)
                sp.dma_start(acc[:, bass.ds(TPG * g, TPG), :], x_v[:, bass.ds(TPG * g, TPG), :]).then_inc(s_x[c], 16)
                if i is None or i >= 2:
                    sp.wait_ge(s_isrel, g - 1)
                sp.dma_start(adj_sb[:, c, :].rearrange("p (t n) -> p t n", n=NODES),
                             adj_v[:, bass.ds(TPG * g, TPG), :]).then_inc(s_adj[c], 16)

            for i in range(2):
                load_group(0, i, i)
            sp.dma_start(w1_f[:, :].rearrange("p (e f) -> p e f", e=E + 1), w1.rearrange("e d f -> d e f")).then_inc(s_weights, 16)
            sp.dma_start(w2_f[:, :, :, :].rearrange("p e c d -> p (e c) d"),
                         w2.rearrange("e (c p) d -> p (e c) d", p=P)).then_inc(s_weights, 16)
            with sp.Fori(1, GROUPS // 2) as k:
                load_group(k, 0, None)
                load_group(k, 1, None)

            sp.wait_ge(s_table, 1)
            sp.wait_ge(s_padids, 2)
            for e in range(E):
                row = sp.value_load(first_pad[0:1, e:e + 1], min_val=0, max_val=ROWS - RB)
                sp.dma_start(rows_dram[bass.ds(row, RB), :].rearrange("(h p) w -> p h w", p=P),
                             padrows[:, RH * e:RH * (e + 1), :]).then_inc(s_padded, 16)

            for c in range(2):
                sp.wait_ge(s_sent[c], 16 * TPG * TOP * GROUPS // 2)
            sp.wait_ge(s_spare, 16)
            sp.wait_ge(s_padded, 16 * E)

            def load_tile(k, c, i):
                if i is None or i >= 2:
                    t = 2 * k + c
                    sp.wait_ge(s_xt[c], 16 * k)
                    sp.wait_ge(s_xtT_ps, t - 1)
                    sp.wait_ge(s_xid, t - 1)
                col = rtab[0:1, 2 * k + c:2 * k + c + 1] if i is not None else rtab[0:1, bass.ds(2 * k + c, 1)]
                row = sp.value_load(col, min_val=0, max_val=ROWS - RB)
                sp.dma_start(xt[:, c, :, :], rows_dram[bass.ds(row, RB), :].rearrange("(h p) w -> p h w", p=P)).then_inc(s_xt[c], 16)

            for i in range(2):
                load_tile(0, i, i)
            with sp.Fori(1, RTILES // 2) as k:
                load_tile(k, 0, None)
                load_tile(k, 1, None)

            for c in range(2):
                sp.wait_ge(s_ysent[c], 16 * RH * RTILES // 2)

            def load_results(k, c, i):
                g = 2 * k + c
                if i is None or i >= 2:
                    sp.wait_ge(s_yb[c], 32 * k)
                    sp.wait_ge(s_add, g - 1)
                for j in range(TOP):
                    sp.dma_start(yb[:, c, j, :, :], results_v[:, j, bass.ds(TPG * g, TPG), :]).then_inc(s_yb[c], 16)

            for i in range(2):
                load_results(0, i, i)
            with sp.Fori(1, GROUPS // 2) as k:
                load_results(k, 0, None)
                load_results(k, 1, None)

        @block.gpsimd
        def _(pool):
            nc.gpsimd.memset(padrows[:, :, :], 0.0).then_inc(s_prep, 1)
            nc.gpsimd.memset(diag[:, :, :, :], 0.0).then_inc(s_prep, 1)
            nc.gpsimd.memset(rowbuf[:, :, :, :, :], 0.0).then_inc(s_prep, 1)
            nc.gpsimd.memset(minus_half[:, :], -0.5).then_inc(s_prep, 1)
            pool.wait_ge(s_prep, 4)
            pool.wait_ge(s_const, 16 * CONST_DMAS)
            nc.gpsimd.tensor_copy(padrows[:, :, D:D + 1].bitcast(I32),
                                  plc[:, K_SPARE:K_SPARE + E * RH].rearrange("p (r o) -> p r o", o=1)).then_inc(s_padids, 1)
            pool.wait_ge(s_padids, 1)
            pool.dma_start(rows_dram[E * REGION:ROWS, :].rearrange("(r p) w -> p r w", p=P), padrows[:, :, :]).then_inc(s_spare, 16)
            pool.wait_ge(s_spare, 16)
            nc.gpsimd.tensor_copy(padrows[:, :, D:D + 1].bitcast(I32),
                                  plc[:, K_PAD:K_PAD + E * RH].rearrange("p (r o) -> p r o", o=1)).then_inc(s_padids, 1)

            def body(k, c, i):
                g = 2 * k + c
                if has(i, 0, GROUPS):
                    if i is None or i >= 2:
                        hold(pool, s_lsel, g - 1)
                    nc.gpsimd.memset(sel[:, c, :, :], NEG).then_inc(s_fill, 1)
                if has(i, 2, GROUPS):
                    hold(pool, s_mv1, g + 3)
                    nc.gpsimd.tensor_scalar(ve1[:, c, :], mv1[:, c, :, 1], EPS, None, ALU.add).then_inc(s_ve1, 1)
                    pool.wait_ge(s_ve1, g + 3)
                    nc.gpsimd.tensor_tensor(rstd1[:, c, :], ve1[:, c, :], minus_half[:, :], ALU.pow).then_inc(s_rstd1, 1)
                if has(i, -2, GROUPS):
                    hold(pool, s_pos, g - 1)
                    for t in range(TPG):
                        for j in range(TOP):
                            nc.gpsimd.indirect_dma_start(
                                out=rows_dram[:, :], out_offset=bass.IndirectOffsetOnAxis(ap=pos[:, c, t, j:j + 1], axis=0),
                                in_=rowbuf[:, c, t, j, :], in_offset=None).then_inc(s_sent[c], 16)
                if has(i, 0, GROUPS):
                    hold(pool, s_mv2, g + 1)
                    nc.gpsimd.tensor_scalar(ve2[:, c, :], mv2[:, c, :, 1], EPS, None, ALU.add).then_inc(s_ve2, 1)
                    pool.wait_ge(s_ve2, g + 1)
                    nc.gpsimd.tensor_tensor(rstd2[:, c, :], ve2[:, c, :], minus_half[:, :], ALU.pow).then_inc(s_rstd2, 1)

            pipeline(pool, body, GROUPS, 2, 2)

            def send_results(k, c, i):
                t = 2 * k + c
                hold(pool, s_yt, t + 1)
                for h in range(RH):
                    nc.gpsimd.indirect_dma_start(
                        out=results_dram[:, :], out_offset=bass.IndirectOffsetOnAxis(ap=yid[:, c, h:h + 1], axis=0),
                        in_=yt[:, c, h, :], in_offset=None).then_inc(s_ysent[c], 16)

            with pool.Fori(0, RTILES // 2) as k:
                send_results(k, 0, None)
                send_results(k, 1, None)

        @block.scalar
        def _(act):
            act.wait_ge(s_angle, 7)
            nc.scalar.activation(ang[:, 3, :], ang[:, 2, :], ACT.Sin).then_inc(s_cos, 1)
            nc.scalar.preload_act_table(ACT.Exp)
            act.wait_ge(s_weights, 32)
            nc.scalar.activation(w1_h[:, :, :, :].rearrange("p e c f -> p (e c f)"), w1_f[:, :], ACT.Copy, scale=WS).then_inc(s_w1h, 1)

            def body(k, c, i):
                g = 2 * k + c
                if has(i, 0, GROUPS):
                    act.wait_ge(s_nmax, g + 1)
                    for t in range(TPG):
                        last = nc.scalar.activation(prob[:, c, t, :], lsel[:, c, t, :], ACT.Exp,
                                                    bias=nmax[:, c, t:t + 1], accum_out=psum_p[:, c, t:t + 1])
                    last.then_inc(s_prob, 1)
                if has(i, -1, GROUPS):
                    act.wait_ge(s_x2T_ps, g)
                    nc.scalar.activation(xh[:, bass.ds(GROUP * (g - 1), GROUP)], x2T_ps, ACT.Copy, scale=XS).then_inc(s_xh, 1)
                if has(i, 1, GROUPS):
                    act.wait_ge(s_xnT_ps, g + 2)
                    nc.scalar.activation(xnT[:, 1 - c, :], xnT_ps, ACT.Copy).then_inc(s_xnT, 1)
                if has(i, 0, GROUPS):
                    act.wait_ge(s_prT_ps, g + 1)
                    if i is None or i >= 2:
                        act.wait_ge(s_att_ps, g - 1)
                    src = prT_ps.rearrange("p (t n) -> p t n", n=P)
                    nc.scalar.activation(diag[0:NODES, c, :, 0:NODES], src[0:NODES, :, 0:NODES], ACT.Copy)
                    nc.scalar.activation(diag[NODES:P, c, :, NODES:P], src[0:NODES, :, NODES:P], ACT.Copy).then_inc(s_diag, 1)
                if has(i, -1, GROUPS):
                    act.wait_ge(s_gap, g)
                    nc.scalar.activation(egap[:, 1 - c, :], gap[:, :], ACT.Exp, scale=UNSCALE).then_inc(s_egap, 1)

            act.wait_ge(s_prep, 4)
            pipeline(act, body, GROUPS, 2, 2)

            nc.scalar.preload_act_table(ACT.Gelu)

            def shared(k, c, i):
                u = 2 * k + c
                if i is None or i >= 2:
                    act.wait_ge(s_sh_down, u - 1)
                for f in range(FC):
                    act.wait_ge(s_sh_up, FC * u + f + 1)
                    h = (hid, hid2)[c]
                    nc.scalar.activation(h[:, f, :], bank[:, f, :], ACT.Gelu, bias=b1_f[:, E * FC + f:E * FC + f + 1],
                                         scale=UNSCALE).then_inc(s_sh_hid, 1)

            act.wait_ge(s_scores, SB * GROUPS)
            for i in range(2):
                shared(0, i, i)
            with act.Fori(1, GROUPS // 2) as k:
                shared(k, 0, None)
                shared(k, 1, None)

            act.wait_ge(s_table, 1)

            def body(k, c, i):
                t = 2 * k + c
                if has(i, 1, RTILES):
                    act.wait_ge(s_xtT_ps, t + 2)
                    nc.scalar.activation(xth[:, 1 - c, :], bank[:, 6 + (1 - c), 0:RB], ACT.Copy, scale=XS).then_inc(s_xth, 1)
                if has(i, 0, RTILES):
                    col = etab[0:1, t:t + 1] if i is not None else etab[0:1, bass.ds(t, 1)]
                    e = act.value_load(col, min_val=0, max_val=E)
                    if i is None or i >= 2:
                        act.wait_ge(s_down, t - 1)
                    for f in range(FC):
                        if f % 2 == 0:
                            act.wait_ge(s_up, 2 * t + f // 2 + 1)
                        h = (hid, hid2)[c]
                        last = nc.scalar.activation(h[:, f, 0:RB], bank[:, 2 * c + f // 2, RB * (f % 2):RB * (f % 2 + 1)], ACT.Gelu,
                                                    bias=b1_f[:, bass.ds(e * FC + f, 1)], scale=UNSCALE)
                    last.then_inc(s_hid, 1)

            act.wait_ge(s_sh_down, GROUPS)
            pipeline(act, body, RTILES, 1, 0)

            def store(k, c, i):
                g = 2 * k + c
                act.wait_ge(s_add, g + 1)
                act.dma_start(out_v[:, bass.ds(TPG * g, TPG), :], acc[:, bass.ds(TPG * g, TPG), :]).then_inc(s_out, 16)

            with act.Fori(0, GROUPS // 2) as k:
                store(k, 0, None)
                store(k, 1, None)
            act.wait_ge(s_out, 16 * GROUPS)

        @block.vector
        def _(dve):
            V = nc.vector
            dve.wait_ge(s_const, 16 * CONST_DMAS)
            V.tensor_copy(tri[:, :], cst[:, C_TRI:C_TRI + P])
            V.memset(ones[:, :], 1.0)
            V.memset(ones_f[:, :], 1.0)
            V.memset(count[:, 0, :], 0.0)
            V.tensor_copy(place[:, :, :].rearrange("p t k -> p (t k)"), plc[:, K_PLACE:K_PLACE + TPG * TOP])
            V.tensor_scalar(wr_h[:, :], wr_f[:, :], WS, None, ALU.mult).then_inc(s_setup, 1)
            dve.wait_ge(s_setup, 1)
            V.scalar_tensor_tensor(wr_l[:, :], wr_f[:, :], WS, wr_h[:, :], ALU.mult, ALU.subtract).then_inc(s_setup, 1)
            V.tensor_scalar(ang[:, 0, :], cst[0:TIMES, C_REL:C_REL + RELATIONS], tw[:, 0:1], None, ALU.mult).then_inc(s_angle, 1)
            dve.wait_ge(s_angle, 1)
            V.tensor_scalar(ang[:, 1, :], ang[:, 0, :], 1.0 / TWO_PI, MAGIC, ALU.mult, ALU.add).then_inc(s_angle, 1)
            dve.wait_ge(s_angle, 2)
            V.tensor_scalar(ang[:, 2, :], ang[:, 1, :], MAGIC, None, ALU.subtract).then_inc(s_angle, 1)
            dve.wait_ge(s_angle, 3)
            V.scalar_tensor_tensor(ang[:, 0, :], ang[:, 2, :], -PI_HI, ang[:, 0, :], ALU.mult, ALU.add).then_inc(s_angle, 1)
            dve.wait_ge(s_angle, 4)
            V.scalar_tensor_tensor(ang[:, 0, :], ang[:, 2, :], -PI_MID, ang[:, 0, :], ALU.mult, ALU.add).then_inc(s_angle, 1)
            dve.wait_ge(s_angle, 5)
            V.scalar_tensor_tensor(ang[:, 0, :], ang[:, 2, :], -PI_LO, ang[:, 0, :], ALU.mult, ALU.add).then_inc(s_angle, 1)
            dve.wait_ge(s_angle, 6)
            V.scalar_tensor_tensor(ang[:, 1, :], ang[:, 0, :], -1.0, ang[:, 0, :], ALU.mult, ALU.max).then_inc(s_trow, 1)
            dve.wait_ge(s_trow, 1)
            V.tensor_scalar(ang[:, 2, :], ang[:, 1, :], -1.0, HALF_PI, ALU.mult, ALU.add).then_inc(s_angle, 1)
            dve.wait_ge(s_cos, 1)
            V.tensor_tensor(ang[:, 0, :], ang[:, 3, :], trel[:, :], ALU.mult).then_inc(s_tprod, 1)
            dve.wait_ge(s_tsum, 1)
            V.tensor_copy(tsum[:, :], att_ps[:, 0:RELATIONS]).then_inc(s_trow, 1)
            dve.wait_ge(s_trow, 2)
            V.tensor_copy(tparts[:, 0, :], tsum[:, :]).then_inc(s_trow, 1)
            dve.wait_ge(s_trow, 3)
            V.tensor_tensor(trest[:, 0, :], tsum[:, :], tparts[:, 0, :], ALU.subtract).then_inc(s_trow, 1)
            dve.wait_ge(s_trow, 4)
            V.tensor_copy(tparts[:, 1, :], trest[:, 0, :]).then_inc(s_trow, 1)
            dve.wait_ge(s_trow, 5)
            V.tensor_tensor(tparts[:, 2, :], trest[:, 0, :], tparts[:, 1, :], ALU.subtract).then_inc(s_trow, 1)
            dve.wait_ge(s_trow, 6)
            V.tensor_scalar(trow[:, 0, :], tparts[:, 0, :], cst[:, C_PART:C_PART + 1], None, ALU.mult).then_inc(s_trow, 1)
            dve.wait_ge(s_trow, 7)
            V.scalar_tensor_tensor(trow[:, 1, :], tparts[:, 1, :], cst[:, C_PART + 1:C_PART + 2], trow[:, 0, :],
                                   ALU.mult, ALU.add).then_inc(s_trow, 1)
            dve.wait_ge(s_trow, 8)
            V.scalar_tensor_tensor(trow[:, 2, :], tparts[:, 2, :], cst[:, C_PART + 2:C_PART + 3], trow[:, 1, :],
                                   ALU.mult, ALU.add).then_inc(s_trow, 1)
            dve.wait_ge(s_trow, 9)
            V.tensor_copy(time_rows[:, :, :], trow[:, 2, :].unsqueeze(2).to_broadcast([P, RELATIONS, GN])).then_inc(s_time, 1)

            def body(k, c, i):
                g = 2 * k + c
                o = 1 - c
                if has(i, 0, GROUPS):
                    dve.wait_ge(s_fill, g + 1)
                    for r in range(RELATIONS):
                        if r % 2 == 0:
                            hold(dve, s_scores, SB * g + r // 2 + 1)
                        if r > 0:
                            hold(dve, s_picked, RELATIONS * g + r)
                        V.copy_predicated(sel[:, c, :, :].rearrange("p t n -> p (t n)"), is_rel[:, c, r, :],
                                          bank[:, r // 2, GN * (r % 2):GN * (r % 2 + 1)]).then_inc(s_picked, 1)
                    dve.wait_ge(s_picked, RELATIONS * (g + 1))
                    V.scalar_tensor_tensor(lsel[:, c, :, :], sel[:, c, :, :], SLOPE, sel[:, c, :, :],
                                           ALU.mult, ALU.max).then_inc(s_lsel, 1)
                    dve.wait_ge(s_lsel, g + 1)
                    V.tensor_reduce(nmax[:, c, :], lsel[:, c, :, :], AX.X, ALU.max, negate=True).then_inc(s_nmax, 1)
                if has(i, -1, GROUPS):
                    dve.wait_ge(s_rstd2, g)
                    if i is None or i >= 3:
                        dve.wait_ge(s_sent[o], 16 * TPG * TOP * (k - 1 + c))
                    for t in range(TPG):
                        V.tensor_scalar(rowbuf[:, o, t, :, 0:D], acc[:, bass.ds(TPG * (g - 1) + t, 1), :].to_broadcast([P, TOP, D]),
                                        mv2[:, o, t, 0:1], rstd2[:, o, t:t + 1], ALU.subtract, ALU.mult)
                    V.tensor_copy(rowbuf[:, o, :, :, D].bitcast(I32), place[:, :, :]).then_inc(s_xn2, 1)
                    dve.wait_ge(s_xn2, g)
                    V.tensor_scalar(place[:, :, :], place[:, :, :], float(GROUP), None, ALU.add).then_inc(s_placed, 1)
                if has(i, 1, GROUPS):
                    dve.wait_ge(s_rstd1, g + 2)
                    for t in range(TPG):
                        last = V.tensor_scalar(xn[:, o, t, :], acc[:, bass.ds(TPG * (g + 1) + t, 1), :].rearrange("p a d -> p (a d)"),
                                               mv1[:, o, t, 0:1], rstd1[:, o, t:t + 1], ALU.subtract, ALU.mult)
                    last.then_inc(s_xn, 1)
                    dve.wait_ge(s_adj[o], 16 * (k + c + 1))
                    for r in range(RELATIONS):
                        last = V.tensor_scalar(is_rel[:, o, r, :], adj_sb[:, o, :], float(r + 1), None, ALU.is_equal)
                    last.then_inc(s_isrel, 1)
                if has(i, -2, GROUPS):
                    dve.wait_ge(s_rank, g - 1)
                    V.tensor_tensor(slot[:, :, :], rank_ps, cst[:, C_REGION:C_REGION + E].unsqueeze(1).to_broadcast([P, TPG, E]),
                                    ALU.add).then_inc(s_slot, 1)
                    dve.wait_ge(s_slot, g - 1)
                    V.tensor_tensor(slot2[:, :, :, :], onehot[:, c, :, :, :], slot[:, :, :].unsqueeze(2).to_broadcast([P, TPG, TOP, E]),
                                    ALU.mult).then_inc(s_slot2, 1)
                    dve.wait_ge(s_slot2, g - 1)
                    with nc.allow_low_precision(reason="whole numbers below 2**24, summed in float32"):
                        V.tensor_reduce(pos[:, c, :, :], slot2[:, :, :, :], AX.X, ALU.add).then_inc(s_pos, 1)
                if has(i, 0, GROUPS):
                    dve.wait_ge(s_prob, g + 1)
                    V.reciprocal(rsum[:, c, :], psum_p[:, c, :]).then_inc(s_rsum, 1)
                if has(i, -1, GROUPS):
                    dve.wait_ge(s_xh, g)
                    cols = bass.ds(GROUP * (g - 1), GROUP)
                    V.scalar_tensor_tensor(xl[:, cols], x2T_ps, XS, xh[:, cols], ALU.mult, ALU.subtract).then_inc(s_xl, 1)
                if has(i, 2, GROUPS):
                    hold(dve, s_x[c], 16 * (k + 2))
                    for t in range(TPG):
                        last = V.bn_stats(st1[:, c, t, :], acc[:, bass.ds(TPG * (g + 2) + t, 1), :].rearrange("p a d -> p (a d)"))
                    last.then_inc(s_bn1, 1)
                    hold(dve, s_bn1, g + 3)
                    for t in range(TPG):
                        last = V.bn_aggr(mv1[:, c, t, :], st1[:, c, t, :])
                    last.then_inc(s_mv1, 1)
                if has(i, 1, GROUPS):
                    dve.wait_ge(s_xnT, g + 2)
                    if i is None or i >= 0:
                        dve.wait_ge(s_scores, SB * (g + 1))
                    for r in range(RELATIONS):
                        last = V.tensor_scalar(axT[:, r, :], xnT[:, o, :], arel[:, r:r + 1], None, ALU.mult)
                    last.then_inc(s_axT, 1)
                if has(i, 0, GROUPS):
                    dve.wait_ge(s_att_ps, g + 1)
                    dve.wait_ge(s_rsum, g + 1)
                    for t in range(TPG):
                        a = acc[:, bass.ds(TPG * g + t, 1), :].rearrange("p a d -> p (a d)")
                        last = V.scalar_tensor_tensor(a, att_ps[:, t * D:(t + 1) * D], rsum[:, c, t:t + 1], a, ALU.mult, ALU.add)
                    last.then_inc(s_after, 1)
                    hold(dve, s_after, g + 1)
                    for t in range(TPG):
                        last = V.bn_stats(st2[:, c, t, :], acc[:, bass.ds(TPG * g + t, 1), :].rearrange("p a d -> p (a d)"))
                    last.then_inc(s_bn2, 1)
                    hold(dve, s_bn2, g + 1)
                    for t in range(TPG):
                        last = V.bn_aggr(mv2[:, c, t, :], st2[:, c, t, :])
                    last.then_inc(s_mv2, 1)
                if has(i, -1, GROUPS):
                    dve.wait_ge(s_router, g)
                    V.tensor_copy(logit[:, :, :], router_ps).then_inc(s_logit, 1)
                    hold(dve, s_logit, g)
                    for t in range(TPG):
                        last = V.max(top8[:, t, :], logit[:, t, :])
                    last.then_inc(s_top8, 1)
                    hold(dve, s_top8, g)
                    V.tensor_tensor(gap[:, :], top8[:, :, 1], top8[:, :, 0], ALU.subtract).then_inc(s_gap, 1)
                    for t in range(TPG):
                        last = V.max_index(idx8[:, t, :], top8[:, t, :], logit[:, t, :])
                    last.then_inc(s_idx8, 1)
                    dve.wait_ge(s_idx8, g)
                    V.tensor_copy(idxf[:, :, :], idx8[:, :, 0:TOP]).then_inc(s_idxf, 1)
                    dve.wait_ge(s_idxf, g)
                    V.tensor_tensor(onehot[:, o, :, :, :], idxf[:, :, :].unsqueeze(3).to_broadcast([P, TPG, TOP, E]),
                                    cst[:, C_IOTA:C_IOTA + E].unsqueeze(1).unsqueeze(1).to_broadcast([P, TPG, TOP, E]),
                                    ALU.is_equal).then_inc(s_onehot, 1)
                    dve.wait_ge(s_onehot, g)
                    V.tensor_tensor(chosen[:, o, :, :], onehot[:, o, :, 0, :], onehot[:, o, :, 1, :], ALU.add).then_inc(s_chosen, 1)
                    dve.wait_ge(s_chosen, g)
                    V.tensor_reduce(count_g[:, :], chosen[:, o, :, :].rearrange("p t e -> p e t"), AX.X, ALU.add).then_inc(s_count_g, 1)
                    dve.wait_ge(s_count_g, g)
                    V.tensor_tensor(count[:, c, :], count[:, o, :], count_g[:, :], ALU.add).then_inc(s_count, 1)
                    dve.wait_ge(s_egap, g)
                    V.tensor_scalar(e1[:, :], egap[:, o, :], 1.0, None, ALU.add).then_inc(s_e1, 1)
                    dve.wait_ge(s_e1, g)
                    V.reciprocal(gates[:, bass.ds(TPG * (g - 1), TPG), 0], e1[:, :]).then_inc(s_gate0, 1)
                    dve.wait_ge(s_gate0, g)
                    V.tensor_tensor(gates[:, bass.ds(TPG * (g - 1), TPG), 1], gates[:, bass.ds(TPG * (g - 1), TPG), 0], egap[:, o, :],
                                    ALU.mult).then_inc(s_gates, 1)

            pipeline(dve, body, GROUPS, 2, 2)

            dve.wait_ge(s_total_ps, 1)
            V.tensor_copy(total[:, :], total_ps).then_inc(s_tab, 1)
            dve.wait_ge(s_tab, 1)
            V.tensor_tensor(first_pad[:, :], total[:, :], cst[:, C_REGION:C_REGION + E], ALU.add)
            V.tensor_scalar(total_i[:, :], total[:, :], float(RB - 1), None, ALU.add).then_inc(s_tab, 1)
            dve.wait_ge(s_tab, 2)
            V.tensor_scalar(n_i[:, :], total_i[:, :], RB.bit_length() - 1, None, ALU.logical_shift_right).then_inc(s_tab, 1)
            dve.wait_ge(s_tab, 3)
            V.tensor_copy(n_f[:, :], n_i[:, :]).then_inc(s_tab, 1)
            prev, done = n_f[:, :], 4
            for step in range(3):
                w = 1 << step
                dve.wait_ge(s_tab, done)
                V.tensor_copy(cum[:, step, 0:w], prev[:, 0:w])
                V.tensor_tensor(cum[:, step, w:E], prev[:, w:E], prev[:, 0:E - w], ALU.add).then_inc(s_tab, 1)
                prev, done = cum[:, step, :], done + 1
            dve.wait_ge(s_tab, 7)
            V.tensor_tensor(past[:, :, :], cst[0:1, C_TILE:C_TILE + RTILES].unsqueeze(2).to_broadcast([1, RTILES, E]),
                            cum[0:1, 2, :].unsqueeze(1).to_broadcast([1, RTILES, E]), ALU.is_ge).then_inc(s_tab, 1)
            dve.wait_ge(s_tab, 8)
            V.tensor_reduce(tile_e[:, :], past[:, :, :], AX.X, ALU.add)
            V.tensor_tensor(past_n[:, :, :], past[:, :, :], n_f[0:1, :].unsqueeze(1).to_broadcast([1, RTILES, E]), ALU.mult).then_inc(s_tab, 1)
            dve.wait_ge(s_tab, 9)
            V.tensor_reduce(tile_b[:, :], past_n[:, :, :], AX.X, ALU.add).then_inc(s_tab, 1)
            dve.wait_ge(s_tab, 10)
            V.tensor_copy(etab[:, :], tile_e[:, :])
            V.tensor_tensor(tile_r[:, :], cst[0:1, C_TILE:C_TILE + RTILES], tile_b[:, :], ALU.subtract).then_inc(s_tab, 1)
            dve.wait_ge(s_tab, 11)
            V.tensor_scalar(tile_b[:, :], tile_e[:, :], float(REGION), None, ALU.mult).then_inc(s_tab, 1)
            dve.wait_ge(s_tab, 12)
            V.scalar_tensor_tensor(rtab[:, :], tile_r[:, :], float(RB), tile_b[:, :], ALU.mult, ALU.add).then_inc(s_table, 1)

            dve.wait_ge(s_w1h, 1)
            V.scalar_tensor_tensor(w1_l[:, :, :, :].rearrange("p e c f -> p (e c f)"), w1_f[:, :], WS,
                                   w1_h[:, :, :, :].rearrange("p e c f -> p (e c f)"), ALU.mult, ALU.subtract).then_inc(s_w1l, 1)

            def shared(k, c, i):
                u = 2 * k + c
                a = acc[:, bass.ds(TPG * u, TPG), :]
                V.tensor_tensor(a, a, b2_f[:, E, :].unsqueeze(1).to_broadcast([P, TPG, D]), ALU.add).then_inc(s_sh_bias, 1)
                dve.wait_ge(s_sh_bias, u + 1)
                dve.wait_ge(s_sh_down, u + 1)
                V.tensor_tensor(a, bank[:, 4 + c, :].rearrange("p (t d) -> p t d", d=D), a, ALU.add).then_inc(s_sh_acc, 1)

            with dve.Fori(0, GROUPS // 2) as k:
                shared(k, 0, None)
                shared(k, 1, None)

            def body(k, c, i):
                t = 2 * k + c
                o = 1 - c
                if has(i, 1, RTILES):
                    dve.wait_ge(s_xth, t + 2)
                    V.scalar_tensor_tensor(xtl[:, o, :], bank[:, 6 + o, 0:RB], XS, xth[:, o, :], ALU.mult, ALU.subtract).then_inc(s_xtl, 1)
                if has(i, -1, RTILES):
                    col = etab[0:1, t - 1:t] if i is not None else etab[0:1, bass.ds(t - 1, 1)]
                    e = dve.value_load(col, min_val=0, max_val=E)
                    if i is None or i >= 3:
                        dve.wait_ge(s_ysent[o], 16 * RH * (k + c - 1))
                    dve.wait_ge(s_xid, t)
                    V.tensor_copy(yid[:, o, :], xid[:, o, :])
                    dve.wait_ge(s_down, t)
                    V.tensor_tensor(yt[:, o, :, :], bank[:, 4 + o, 0:RH * D].rearrange("p (h d) -> p h d", d=D),
                                    b2_f[:, bass.ds(e, 1), :].to_broadcast([P, RH, D]), ALU.add).then_inc(s_yt, 1)
                if has(i, 1, RTILES):
                    dve.wait_ge(s_xt[o], 16 * (k + c + 1))
                    if i is None or i >= 1:
                        dve.wait_ge(s_yt, t)
                    V.tensor_copy(xid[:, o, :], xt[:, o, :, D].bitcast(I32)).then_inc(s_xid, 1)

            pipeline(dve, body, RTILES, 1, 1)

            def combine(k, c, i):
                g = 2 * k + c
                dve.wait_ge(s_yb[c], 32 * (k + 1))
                for j in range(TOP):
                    for t in range(TPG):
                        a = acc[:, bass.ds(TPG * g + t, 1), :].rearrange("p a d -> p (a d)")
                        last = V.scalar_tensor_tensor(a, yb[:, c, j, t, :], gates[:, bass.ds(TPG * g + t, 1), j], a, ALU.mult, ALU.add)
                    last.then_inc((s_add0, s_add)[j], 1)
                    if j == 0:
                        dve.wait_ge(s_add0, g + 1)

            with dve.Fori(0, GROUPS // 2) as k:
                combine(k, 0, None)
                combine(k, 1, None)

        @block.tensor
        def _(pe):
            MM = nc.tensor.matmul
            pe.wait_ge(s_setup, 2)
            pe.wait_ge(s_tprod, 1)
            MM(att_ps[:, 0:RELATIONS], ones_f[:, :], ang[:, 0, :], start=True, stop=True).then_inc(s_tsum, 1)
            pe.wait_ge(s_time, 1)

            def body(k, c, i):
                g = 2 * k + c
                o = 1 - c
                if has(i, 0, GROUPS):
                    pe.wait_ge(s_axT, g + 1)
                    for q in range(SB):
                        rels = range(2 * q, min(2 * q + 2, RELATIONS))
                        w = len(rels) * GN
                        if i is None or i >= 1:
                            pe.wait_ge(s_picked, RELATIONS * (g - 1) + rels[-1] + 1)
                        for n in range(2 * TPG):
                            half = slice(n % 2 * NODES, (n % 2 + 1) * NODES)
                            out_ps = bank[half, q, 0:w].rearrange("p (r t n) -> p r t n", t=TPG, n=NODES)[:, :, n // 2, :]
                            MM(out_ps, xnT[:, c, n * NODES:(n + 1) * NODES],
                                      axT[:, rels[0]:rels[-1] + 1, n * NODES:(n + 1) * NODES], start=(n < 2),
                                      stop=False, skip_group_check=True)
                        last = MM(bank[:, q, 0:w], ones[:, :], time_rows[:, rels[0]:rels[-1] + 1, :].rearrange("p r n -> p (r n)"),
                                  start=False, stop=True, skip_group_check=True)
                        last.then_inc(s_scores, 1)
                if has(i, -2, GROUPS):
                    pe.wait_ge(s_count, g - 1)
                    MM(rank_ps, tri[:, :], chosen[:, c, :, :], start=True, stop=False)
                    for t in range(TPG - 1):
                        MM(rank_ps[:, t + 1:TPG, :], ones[:, :], chosen[:, c, t:t + 1, :].to_broadcast([P, TPG - 1 - t, E]), start=False, stop=False)
                    MM(rank_ps, ones[:, :], count[:, c:c + 1, :].to_broadcast([P, TPG, E]), start=False, stop=True).then_inc(s_rank, 1)
                if has(i, -1, GROUPS):
                    pe.wait_ge(s_xn2, g)
                    if i is None or i >= 2:
                        pe.wait_ge(s_xl, g - 1)
                    for t in range(TPG):
                        last = nc.tensor.transpose(x2T_ps[:, t * P:(t + 1) * P], rowbuf[:, o, t, 0, 0:D], ident)
                    last.then_inc(s_x2T_ps, 1)
                if has(i, 1, GROUPS):
                    pe.wait_ge(s_xn, g + 2)
                    if i is None or i >= 0:
                        pe.wait_ge(s_xnT, g + 1)
                    for t in range(TPG):
                        last = nc.tensor.transpose(xnT_ps[:, t * P:(t + 1) * P], xn[:, o, t, :], ident)
                    last.then_inc(s_xnT_ps, 1)
                if has(i, 0, GROUPS):
                    hold(pe, s_prob, g + 1)
                    for t in range(TPG):
                        last = nc.tensor.transpose(prT_ps[0:NODES, t * P:(t + 1) * P], prob[:, c, t, :], ident)
                    last.then_inc(s_prT_ps, 1)
                    pe.wait_ge(s_diag, g + 1)
                    if i is None or i >= 1:
                        pe.wait_ge(s_after, g)
                    for t in range(TPG):
                        last = MM(att_ps[:, t * D:(t + 1) * D], diag[:, c, t, :], xn[:, c, t, :], start=True, stop=True)
                    last.then_inc(s_att_ps, 1)
                if has(i, -1, GROUPS):
                    pe.wait_ge(s_xl, g)
                    if i is None or i >= 2:
                        pe.wait_ge(s_slot, g - 1)
                    for t in range(TPG):
                        cols = bass.ds(GROUP * (g - 1) + t * P, P)
                        MM(router_ps[:, t, :], xh[:, cols], wr_h[:, :], start=True, stop=False)
                        MM(router_ps[:, t, :], xh[:, cols], wr_l[:, :], start=False, stop=False)
                        last = MM(router_ps[:, t, :], xl[:, cols], wr_h[:, :], start=False, stop=True)
                    last.then_inc(s_router, 1)

            pipeline(pe, body, GROUPS, 2, 2)

            pe.wait_ge(s_count, GROUPS)
            pe.wait_ge(s_pos, GROUPS)
            MM(total_ps, ones[:, :], count[:, GROUPS % 2, :], start=True, stop=True).then_inc(s_total_ps, 1)
            pe.wait_ge(s_w1l, 1)

            def up(k, c, i):
                u = 2 * k + c
                for f in range(FC):
                    if i != 0:
                        pe.wait_ge(s_sh_hid, FC * (u - 1) + f + 1)
                    xs = (xh[:, bass.ds(GROUP * u, GROUP)], xl[:, bass.ds(GROUP * u, GROUP)])
                    MM(bank[:, f, :], w1_h[:, E, f, :], xs[0], start=True, stop=False)
                    MM(bank[:, f, :], w1_h[:, E, f, :], xs[1], start=False, stop=False)
                    MM(bank[:, f, :], w1_l[:, E, f, :], xs[0], start=False, stop=True).then_inc(s_sh_up, 1)

            def down(k, c, i):
                u = 2 * k + c
                pe.wait_ge(s_sh_hid, FC * (u + 1))
                if i is None or i >= 2:
                    pe.wait_ge(s_sh_acc, u - 1)
                for t in range(TPG):
                    for f in range(FC):
                        last = MM(bank[:, 4 + c, t * D:(t + 1) * D], (hid, hid2)[c][:, f, t * P:(t + 1) * P], w2_f[:, E, f, :],
                                  start=(f == 0), stop=(f == FC - 1))
                last.then_inc(s_sh_down, 1)

            up(0, 0, 0)
            up(0, 1, 1)
            down(0, 0, 0)
            with pe.Fori(1, GROUPS // 2) as k:
                up(k, 0, None)
                down(k - 1, 1, 2)
                up(k, 1, None)
                down(k, 0, None)
            down(GROUPS // 2 - 1, 1, GROUPS - 1)
            pe.wait_ge(s_sh_acc, GROUPS)

            def body(k, c, i):
                t = 2 * k + c
                o = 1 - c
                if has(i, 1, RTILES):
                    pe.wait_ge(s_xt[o], 16 * (k + c + 1))
                    if i is None or i >= 1:
                        pe.wait_ge(s_xtl, t)
                    for h in range(RH):
                        last = nc.tensor.transpose(bank[:, 6 + o, h * P:(h + 1) * P], xt[:, o, h, 0:D], ident)
                    last.then_inc(s_xtT_ps, 1)
                if has(i, 0, RTILES):
                    col = etab[0:1, t:t + 1] if i is not None else etab[0:1, bass.ds(t, 1)]
                    e = pe.value_load(col, min_val=0, max_val=E)
                    pe.wait_ge(s_xtl, t + 1)
                    if i is None or i >= 2:
                        pe.wait_ge(s_hid, t - 1)
                    for f in range(FC):
                        ps = bank[:, 2 * c + f // 2, RB * (f % 2):RB * (f % 2 + 1)]
                        wh = w1_h[:, bass.ds(e, 1), f, :].rearrange("p a f -> p (a f)")
                        wl = w1_l[:, bass.ds(e, 1), f, :].rearrange("p a f -> p (a f)")
                        MM(ps, wh, xth[:, c, :], start=True, stop=False)
                        MM(ps, wh, xtl[:, c, :], start=False, stop=False)
                        last = MM(ps, wl, xth[:, c, :], start=False, stop=True)
                        if f % 2:
                            last.then_inc(s_up, 1)
                if has(i, -1, RTILES):
                    col = etab[0:1, t - 1:t] if i is not None else etab[0:1, bass.ds(t - 1, 1)]
                    e = pe.value_load(col, min_val=0, max_val=E)
                    pe.wait_ge(s_hid, t)
                    if i is None or i >= 3:
                        pe.wait_ge(s_yt, t - 2)
                    for h in range(RH):
                        for f in range(FC):
                            last = MM(bank[:, 4 + o, h * D:(h + 1) * D], (hid, hid2)[o][:, f, h * P:(h + 1) * P],
                                      w2_f[:, bass.ds(e, 1), f, :].rearrange("p a d -> p (a d)"), start=(f == 0), stop=(f == FC - 1))
                    last.then_inc(s_down, 1)

            pe.wait_ge(s_table, 1)
            pipeline(pe, body, RTILES, 1, 1)


def kernel(**inputs):
    import numpy as np
    from concourse import bacc
    from concourse.bass_utils import run_bass_kernel_spmd

    g = {name.replace("L0_gnn_", "").replace("L0_ffn_", ""): np.asarray(a) for name, a in inputs.items()}
    p = np.arange(P)
    constants = np.zeros((P, C_ALL), np.float32)
    constants[:, C_IDENT:C_IDENT + P] = np.eye(P)
    constants[:, C_TRI:C_TRI + P] = p[:, None] < p[None, :]
    constants[:, C_IOTA:C_IOTA + E] = np.arange(E)
    constants[:, C_REGION:C_REGION + E] = np.arange(E) * REGION
    constants[:, C_PART:C_PART + 3] = np.eye(P)[:, 0:3]
    constants[:, C_REL:C_REL + RELATIONS] = np.arange(1, RELATIONS + 1)
    constants[:, C_TILE:C_TILE + RTILES] = np.arange(RTILES)
    places = np.zeros((P, K_ALL), np.int32)
    t, k = np.meshgrid(np.arange(TPG), np.arange(TOP), indexing="ij")
    places[:, K_PLACE:K_PLACE + TPG * TOP] = p[:, None] + (t * P + k * TOKENS).reshape(1, -1)
    places[:, K_PAD:K_PAD + E * RH] = TOP * TOKENS + p[:, None] + P * np.arange(E * RH)
    places[:, K_SPARE:K_SPARE + E * RH] = TOP * TOKENS + E * RB + p[:, None] + P * np.arange(E * RH)

    def chunks(b):
        return np.ascontiguousarray(b.reshape(-1, P).T)

    arrays = {
        "x": g["x"].reshape(TOKENS, D),
        "adj": g["adj"].reshape(TOKENS, NODES),
        "a_relT": np.ascontiguousarray(g["a_rel"].T),
        "t_relT": np.ascontiguousarray(g["t_rel"].T),
        "time_w": g["time_w"].reshape(TIMES, 1),
        "wr": g["Wr"],
        "w1": np.concatenate([g["W1p"], g["W1s"][None]]),
        "w2": np.concatenate([g["W2p"], g["W2s"][None]]),
        "b1T": chunks(np.concatenate([g["b1p"].reshape(-1), g["b1s"]])),
        "b2": np.ascontiguousarray(np.broadcast_to(np.concatenate([g["b2p"].reshape(-1), g["b2s"]]), (P, (E + 1) * D))),
        "constants": constants,
        "places": places,
    }
    nc = bacc.Bacc("TRN2", target_bir_lowering=False, num_devices=1)
    args = [nc.dram_tensor(n, a.shape, mybir.dt.from_np(a.dtype), kind="ExternalInput").ap() for n, a in arrays.items()]
    out = nc.dram_tensor("out", (TOKENS, D), F32, kind="ExternalOutput").ap()
    rows = nc.dram_tensor("expert_rows", (ROWS, RW), F32, kind="Internal").ap()
    results = nc.dram_tensor("expert_results", (YROWS, D), F32, kind="Internal").ap()
    build(nc, *args, out, rows, results)
    r = run_bass_kernel_spmd(nc, [arrays], core_ids=[0])
    return r.results[0]["out"].reshape(GRAPHS, NODES, D)
```

```python
from contextlib import ExitStack

import concourse.bass as bass
from concourse import mybir

F32 = mybir.dt.float32
F16 = mybir.dt.float16
BF16 = mybir.dt.bfloat16
I32 = mybir.dt.int32
U32 = mybir.dt.uint32
ALU = mybir.AluOpType
ACT = mybir.ActivationFunctionType
AX = mybir.AxisListType

P = 128
GRAPHS, NODES, D = 128, 64, 128
TOKENS = GRAPHS * NODES
RELATIONS = 5
TIMES = 64
E = 8
F = 512
FC = F // P
TOP = 2
TPG = 4
GROUP = TPG * P
GROUPS = TOKENS // GROUP
TILES = TOKENS // P
GN = TPG * NODES
SB = (RELATIONS + 1) // 2
RB = 256
RH = RB // P
REGION = TOKENS + RB
RTILES = TOP * TOKENS // RB + E
ROWS = E * REGION + E * RB
RW = D + 2
YROWS = TOP * TOKENS + 2 * E * RB
EPS = 1e-5
NEG = -9000000000000000.0
SLOPE = 0.2
XS = 2.0 ** 6
WS = 2.0 ** 8
UNSCALE = 1.0 / (XS * WS)
TWO_PI = 6.283185307179586
PI_HI = 6.28125
PI_MID = 0.0019350051879882812
PI_LO = 3.0199159819597e-07
HALF_PI = TWO_PI / 4
MAGIC = 12582912.0

C_IDENT, C_TRI, C_IOTA, C_REGION, C_PART, C_REL, C_TILE = 0, P, 2 * P, 2 * P + E, 2 * P + 2 * E, 2 * P + 2 * E + 3, 2 * P + 2 * E + 3 + RELATIONS
C_ALL = C_TILE + RTILES
K_PLACE, K_PAD, K_SPARE = 0, TPG * TOP, TPG * TOP + E * RH
K_ALL = K_SPARE + E * RH


def build(nc, x, adj, a_relT, t_relT, time_w, wr, w1, w2, b1T, b2, constants, places, out, rows_dram, results_dram):
    x_v = x.rearrange("(t p) d -> p t d", p=P)
    adj_v = adj.rearrange("(t p) n -> p t n", p=P)
    out_v = out.rearrange("(t p) d -> p t d", p=P)
    results_v = results_dram[0:TOP * TOKENS, :].rearrange("(k t p) d -> p k t d", p=P, k=TOP)

    with ExitStack() as ctx:
        def sb(name, shape, dt):
            return ctx.enter_context(nc.sbuf_tensor(name, shape, dt))

        def sem(name):
            return ctx.enter_context(nc.semaphore(name))

        cst = sb("cst", [P, C_ALL], F32)
        plc = sb("plc", [P, K_ALL], I32)
        ident = cst[:, C_IDENT:C_IDENT + P]
        arel = sb("arel", [P, RELATIONS], F32)
        wr_f = sb("wr_f", [P, E], F32)
        wr_h = sb("wr_h", [P, E], F16)
        wr_l = sb("wr_l", [P, E], F16)
        w1_f = sb("w1_f", [P, (E + 1) * F], F32)
        w1_h = sb("w1_h", [P, E + 1, FC, P], F16)
        w1_l = sb("w1_l", [P, E + 1, FC, P], F16)
        w2_f = sb("w2_f", [P, E + 1, FC, D], F32)
        b1_f = sb("b1_f", [P, (E + 1) * FC], F32)
        b2_f = sb("b2_f", [P, E + 1, D], F32)
        tri = sb("tri", [P, P], BF16)
        ones = sb("ones", [P, P], BF16)
        ones_f = sb("ones_f", [TIMES, P], F32)
        minus_half = sb("minus_half", [P, 2, TPG], F32)
        tw = sb("tw", [TIMES, 1], F32)
        trel = sb("trel", [TIMES, RELATIONS], F32)
        ang = sb("ang", [TIMES, 4, RELATIONS], F32)
        tsum = sb("tsum", [P, RELATIONS], F32)
        tparts = sb("tparts", [P, 3, RELATIONS], BF16)
        trest = sb("trest", [P, 2, RELATIONS], F32)
        trow = sb("trow", [P, 3, RELATIONS], F32)
        time_rows = sb("time_rows", [P, RELATIONS, GN], BF16)
        acc = sb("acc", [P, TILES, D], F32)
        xh = sb("xh", [P, TOKENS], F16)
        xl = sb("xl", [P, TOKENS], F16)
        gates = sb("gates", [P, TILES, TOP], F32)
        adj_sb = sb("adj_sb", [P, 2, TPG * NODES], I32)
        is_rel = sb("is_rel", [P, 2, RELATIONS, TPG * NODES], I32)
        stats = sb("stats", [P, 2, 2, TPG, 6], F32)
        mv = sb("mv", [P, 2, 2, TPG, 2], F32)
        var_eps = sb("var_eps", [P, 2, 2, TPG], F32)
        rstd = sb("rstd", [P, 2, 2, TPG], F32)
        shift2 = sb("shift2", [P, TPG], F32)
        xn = sb("xn", [P, 2, TPG, D], F32)
        xnT = sb("xnT", [P, 2, GROUP], F32)
        axT = sb("axT", [P, RELATIONS, GROUP], F32)
        sel = sb("sel", [P, 2, TPG, NODES], F32)
        lsel = sb("lsel", [P, 2, TPG, NODES], F32)
        nmax = sb("nmax", [P, 2, TPG], F32)
        prob = sb("prob", [P, 2, TPG, NODES], F32)
        psum_p = sb("psum_p", [P, 2, TPG], F32)
        rsum = sb("rsum", [P, 2, TPG], F32)
        diag = sb("diag", [P, 2, TPG, P], F32)
        rowbuf = sb("rowbuf", [P, 2, TPG, TOP, RW], F32)
        place = sb("place", [P, TPG, TOP], I32)
        logit = sb("logit", [P, TPG, E], F32)
        top8 = sb("top8", [P, TPG, E], F32)
        idx8 = sb("idx8", [P, TPG, E], U32)
        idxf = sb("idxf", [P, TPG, TOP], F32)
        onehot = sb("onehot", [P, 2, TPG, TOP, E], F32)
        chosen = sb("chosen", [P, 2, TPG, E], BF16)
        count_g = sb("count_g", [P, E], F32)
        count = sb("count", [P, 3, E], BF16)
        gap = sb("gap", [P, TPG], F32)
        egap = sb("egap", [P, 2, TPG], F32)
        e1 = sb("e1", [P, TPG], F32)
        slot = sb("slot", [P, TPG, E], F32)
        slot2 = sb("slot2", [P, TPG, TOP, E], F32)
        pos = sb("pos", [P, 2, TPG, TOP], I32)
        total = sb("total", [P, E], F32)
        total_i = sb("total_i", [P, E], I32)
        first_pad = sb("first_pad", [P, E], I32)
        n_i = sb("n_i", [P, E], I32)
        n_f = sb("n_f", [P, E], F32)
        cum = sb("cum", [P, 3, E], F32)
        past = sb("past", [1, RTILES, E], F32)
        past_n = sb("past_n", [1, RTILES, E], F32)
        tile_e = sb("tile_e", [1, RTILES], F32)
        tile_b = sb("tile_b", [1, RTILES], F32)
        tile_r = sb("tile_r", [1, RTILES], F32)
        etab = sb("etab", [1, RTILES], I32)
        rtab = sb("rtab", [1, RTILES], I32)
        padrows = sb("padrows", [P, E * RH, RW], F32)
        hid = axT[:, 0:FC, :]
        hid2 = sb("hid2", [P, FC, GROUP], F32)
        xt = sb("xt", [P, 2, RH, RW], F32)
        xth = sb("xth", [P, 2, RB], F16)
        xtl = sb("xtl", [P, 2, RB], F16)
        yt = xn[:, :, 0:RH, :]
        xid = sb("xid", [P, 2, RH], I32)
        yid = sb("yid", [P, 2, RH], I32)
        yb = w1_f[:, 0:2 * TOP * TPG * D].rearrange("p (c k t d) -> p c k t d", c=2, k=TOP, t=TPG)

        bank = ctx.enter_context(nc.psum_tensor("bank", [P, 8, 512], F32))

        xnT_ps, x2T_ps, prT_ps, att_ps = (bank[:, b, :] for b in (3, 4, 5, 6))
        router_ps = bank[:, 7, 0:TPG * E].rearrange("p (t e) -> p t e", e=E)
        rank_ps = bank[:, 7, 64:64 + TPG * E].rearrange("p (t e) -> p t e", e=E)
        total_ps = bank[:, 7, 128:128 + E]

        s_const = sem("s_const")
        s_weights = sem("s_weights")
        s_x = [sem("s_x_even"), sem("s_x_odd")]
        s_adj = [sem("s_adj0"), sem("s_adj1")]
        s_held = sem("s_held")
        s_setup = sem("s_setup")
        s_angle = sem("s_angle")
        s_cos = sem("s_cos")
        s_tprod = sem("s_tprod")
        s_tsum = sem("s_tsum")
        s_trow = sem("s_trow")
        s_time = sem("s_time")
        s_prep = sem("s_prep")
        s_w1h = sem("s_w1h")
        s_w1l = sem("s_w1l")
        s_bn1 = sem("s_bn1")
        s_bn2 = sem("s_bn2")
        s_mv = sem("s_mv")
        s_var = sem("s_var")
        s_rstd = sem("s_rstd")
        s_shift = sem("s_shift")
        s_xn = sem("s_xn")
        s_isrel = sem("s_isrel")
        s_xnT_ps = sem("s_xnT_ps")
        s_xnT = sem("s_xnT")
        s_axT = sem("s_axT")
        s_fill = sem("s_fill")
        s_scores = sem("s_scores")
        s_picked = sem("s_picked")
        s_lsel = sem("s_lsel")
        s_nmax = sem("s_nmax")
        s_prob = sem("s_prob")
        s_prT_ps = sem("s_prT_ps")
        s_diag = sem("s_diag")
        s_rsum = sem("s_rsum")
        s_att_ps = sem("s_att_ps")
        s_after = sem("s_after")
        s_xn2 = sem("s_xn2")
        s_ids = sem("s_ids")
        s_x2T_ps = sem("s_x2T_ps")
        s_xh = sem("s_xh")
        s_xl = sem("s_xl")
        s_router = sem("s_router")
        s_logit = sem("s_logit")
        s_top8 = sem("s_top8")
        s_idx8 = sem("s_idx8")
        s_idxf = sem("s_idxf")
        s_onehot = sem("s_onehot")
        s_chosen = sem("s_chosen")
        s_count_g = sem("s_count_g")
        s_count = sem("s_count")
        s_gap = sem("s_gap")
        s_egap = sem("s_egap")
        s_e1 = sem("s_e1")
        s_gate0 = sem("s_gate0")
        s_gates = sem("s_gates")
        s_rank = sem("s_rank")
        s_slot = sem("s_slot")
        s_slot2 = sem("s_slot2")
        s_pos = sem("s_pos")
        s_placed = sem("s_placed")
        s_sent = [sem("s_sent0"), sem("s_sent1")]
        s_spare = sem("s_spare")
        s_padids = sem("s_padids")
        s_padded = sem("s_padded")
        s_total_ps = sem("s_total_ps")
        s_tab = sem("s_tab")
        s_table = sem("s_table")
        s_sh_up = sem("s_sh_up")
        s_sh_hid = sem("s_sh_hid")
        s_sh_down = sem("s_sh_down")
        s_sh_bias = sem("s_sh_bias")
        s_sh_acc = sem("s_sh_acc")
        s_xt = [sem("s_xt0"), sem("s_xt1")]
        s_xtT_ps = sem("s_xtT_ps")
        s_xth = sem("s_xth")
        s_xtl = sem("s_xtl")
        s_up = sem("s_up")
        s_hid = sem("s_hid")
        s_down = sem("s_down")
        s_xid = sem("s_xid")
        s_yt = sem("s_yt")
        s_ysent = [sem("s_ysent0"), sem("s_ysent1")]
        s_yb = [sem("s_yb0"), sem("s_yb1")]
        s_add0 = sem("s_add0")
        s_add = sem("s_add")
        s_out = sem("s_out")

        CONST_DMAS = 8
        block = ctx.enter_context(nc.Block())

        def pipeline(engine, body, n, before, after):
            for i in range(-before, 4):
                body(i // 2, i % 2, i)
            with engine.Fori(2, (n - 2) // 2) as k:
                body(k, 0, None)
                body(k, 1, None)
            for i in range(n - 2, n + after):
                body(i // 2, i % 2, i)

        def hold(engine, semaphore, value):
            engine.wait_ge(semaphore, value)
            engine.sem_inc(s_held, 1)

        def expert(engine, t, i):
            col = etab[0:1, bass.ds(t, 1)] if i is None else etab[0:1, t:t + 1]
            return engine.value_load(col, min_val=0, max_val=E)

        def has(i, d, n):
            return i is None or 0 <= i + d < n

        @block.sync
        def _(sp):
            sp.dma_start(cst[:, :], constants).then_inc(s_const, 16)
            sp.dma_start(plc[:, :], places).then_inc(s_const, 16)
            sp.dma_start(arel[:, :], a_relT).then_inc(s_const, 16)
            sp.dma_start(tw[:, :], time_w).then_inc(s_const, 16)
            sp.dma_start(trel[:, :], t_relT).then_inc(s_const, 16)
            sp.dma_start(wr_f[:, :], wr).then_inc(s_const, 16)
            sp.dma_start(b1_f[:, :], b1T).then_inc(s_const, 16)
            sp.dma_start(b2_f[:, :, :].rearrange("p e d -> p (e d)"), b2).then_inc(s_const, 16)

            def load_group(k, c, i):
                g = 2 * k + c
                if i is None or i >= 2:
                    sp.wait_ge(s_x[c], 16 * k)
                    sp.wait_ge(s_adj[c], 16 * k)
                sp.dma_start(acc[:, bass.ds(TPG * g, TPG), :], x_v[:, bass.ds(TPG * g, TPG), :]).then_inc(s_x[c], 16)
                if i is None or i >= 2:
                    sp.wait_ge(s_isrel, g - 1)
                sp.dma_start(adj_sb[:, c, :].rearrange("p (t n) -> p t n", n=NODES),
                             adj_v[:, bass.ds(TPG * g, TPG), :]).then_inc(s_adj[c], 16)

            for i in range(4):
                load_group(i // 2, i % 2, i)
            sp.dma_start(w1_f[:, :].rearrange("p (e f) -> p e f", e=E + 1), w1.rearrange("e d f -> d e f")).then_inc(s_weights, 16)
            sp.dma_start(w2_f[:, :, :, :].rearrange("p e c d -> p (e c) d"),
                         w2.rearrange("e (c p) d -> p (e c) d", p=P)).then_inc(s_weights, 16)
            with sp.Fori(2, GROUPS // 2) as k:
                load_group(k, 0, None)
                load_group(k, 1, None)

            sp.wait_ge(s_table, 1)
            sp.wait_ge(s_padids, 2)
            for e in range(E):
                row = sp.value_load(first_pad[0:1, e:e + 1], min_val=0, max_val=ROWS - RB)
                sp.dma_start(rows_dram[bass.ds(row, RB), :].rearrange("(h p) w -> p h w", p=P),
                             padrows[:, RH * e:RH * (e + 1), :]).then_inc(s_padded, 16)

            for c in range(2):
                sp.wait_ge(s_sent[c], 16 * TPG * TOP * GROUPS // 2)
            sp.wait_ge(s_spare, 16)
            sp.wait_ge(s_padded, 16 * E)

            def load_tile(k, c, i):
                t = 2 * k + c
                col = rtab[0:1, bass.ds(t, 1)] if i is None else rtab[0:1, t:t + 1]
                row = sp.value_load(col, min_val=0, max_val=ROWS - RB)
                if i is None or i >= 2:
                    hold(sp, s_xt[c], 16 * k)
                    hold(sp, s_xid, t - 1)
                sp.dma_start(xt[:, c, :, :], rows_dram[bass.ds(row, RB), :].rearrange("(h p) w -> p h w", p=P)).then_inc(s_xt[c], 16)

            for i in range(2):
                load_tile(0, i, i)
            with sp.Fori(1, RTILES // 2) as k:
                load_tile(k, 0, None)
                load_tile(k, 1, None)

            for c in range(2):
                sp.wait_ge(s_ysent[c], 16 * RH * RTILES // 2)

            def load_results(k, c, i):
                g = 2 * k + c
                if i is None or i >= 2:
                    sp.wait_ge(s_yb[c], 32 * k)
                    sp.wait_ge(s_add, g - 1)
                for j in range(TOP):
                    sp.dma_start(yb[:, c, j, :, :], results_v[:, j, bass.ds(TPG * g, TPG), :]).then_inc(s_yb[c], 16)

            for i in range(2):
                load_results(0, i, i)
            with sp.Fori(1, GROUPS // 2) as k:
                load_results(k, 0, None)
                load_results(k, 1, None)

        @block.gpsimd
        def _(pool):
            nc.gpsimd.memset(padrows[:, :, :], 0.0).then_inc(s_prep, 1)
            nc.gpsimd.memset(diag[:, :, :, :], 0.0).then_inc(s_prep, 1)
            nc.gpsimd.memset(rowbuf[:, :, :, :, :], 0.0).then_inc(s_prep, 1)
            nc.gpsimd.memset(minus_half[:, :, :], -0.5).then_inc(s_prep, 1)
            pool.wait_ge(s_prep, 4)
            pool.wait_ge(s_const, 16 * CONST_DMAS)
            nc.gpsimd.tensor_copy(padrows[:, :, D:D + 1].bitcast(I32),
                                  plc[:, K_SPARE:K_SPARE + E * RH].rearrange("p (r o) -> p r o", o=1)).then_inc(s_padids, 1)
            pool.wait_ge(s_padids, 1)
            pool.dma_start(rows_dram[E * REGION:ROWS, :].rearrange("(r p) w -> p r w", p=P), padrows[:, :, :]).then_inc(s_spare, 16)
            pool.wait_ge(s_spare, 16)
            nc.gpsimd.tensor_copy(padrows[:, :, D:D + 1].bitcast(I32),
                                  plc[:, K_PAD:K_PAD + E * RH].rearrange("p (r o) -> p r o", o=1)).then_inc(s_padids, 1)

            def body(k, c, i):
                g = 2 * k + c
                if has(i, 1, GROUPS):
                    if i is None or i >= 1:
                        hold(pool, s_lsel, g)
                    nc.gpsimd.memset(sel[:, 1 - c, :, :], NEG).then_inc(s_fill, 1)
                if has(i, -2, GROUPS):
                    hold(pool, s_pos, g - 1)
                    for t in range(TPG):
                        for j in range(TOP):
                            nc.gpsimd.indirect_dma_start(
                                out=rows_dram[:, :], out_offset=bass.IndirectOffsetOnAxis(ap=pos[:, c, t, j:j + 1], axis=0),
                                in_=rowbuf[:, c, t, j, :], in_offset=None).then_inc(s_sent[c], 16)
                if has(i, 0, GROUPS) or has(i, 2, GROUPS):
                    w = slice(0 if has(i, 2, GROUPS) else 1, 2 if has(i, 0, GROUPS) else 1)
                    hold(pool, s_mv, g + 3)
                    nc.gpsimd.tensor_scalar(var_eps[:, c, w, :], mv[:, c, w, :, 1], EPS, None, ALU.add).then_inc(s_var, 1)
                    pool.wait_ge(s_var, g + 3)
                    nc.gpsimd.tensor_tensor(rstd[:, c, w, :], var_eps[:, c, w, :], minus_half[:, w, :], ALU.pow).then_inc(s_rstd, 1)

            pipeline(pool, body, GROUPS, 2, 2)

            def send_results(k, c, i):
                t = 2 * k + c
                hold(pool, s_yt, t + 1)
                for h in range(RH):
                    nc.gpsimd.indirect_dma_start(
                        out=results_dram[:, :], out_offset=bass.IndirectOffsetOnAxis(ap=yid[:, c, h:h + 1], axis=0),
                        in_=yt[:, c, h, :], in_offset=None).then_inc(s_ysent[c], 16)

            with pool.Fori(0, RTILES // 2) as k:
                send_results(k, 0, None)
                send_results(k, 1, None)

        @block.scalar
        def _(act):
            act.wait_ge(s_angle, 7)
            nc.scalar.activation(ang[:, 3, :], ang[:, 2, :], ACT.Sin).then_inc(s_cos, 1)
            nc.scalar.preload_act_table(ACT.Exp)

            def body(k, c, i):
                g = 2 * k + c
                o = 1 - c
                if i == 0:
                    act.wait_ge(s_weights, 32)
                    nc.scalar.activation(w1_h[:, :, :, :].rearrange("p e c f -> p (e c f)"), w1_f[:, :], ACT.Copy, scale=WS).then_inc(s_w1h, 1)
                if has(i, -1, GROUPS):
                    act.wait_ge(s_shift, g)
                    if i is None or i >= 3:
                        act.wait_ge(s_sent[o], 16 * TPG * TOP * (k - 1 + c))
                    for t in range(TPG):
                        last = nc.scalar.activation(rowbuf[:, o, t, :, 0:D], acc[:, bass.ds(TPG * (g - 1) + t, 1), :].to_broadcast([P, TOP, D]),
                                                    ACT.Identity, bias=shift2[:, t:t + 1], scale=rstd[:, o, 1, t:t + 1])
                    last.then_inc(s_xn2, 1)
                if has(i, 1, GROUPS):
                    act.wait_ge(s_xnT_ps, g + 2)
                    nc.scalar.activation(xnT[:, o, :], xnT_ps, ACT.Copy).then_inc(s_xnT, 1)
                    scale_by(k, c, i, range(0, 2))
                if has(i, 0, GROUPS):
                    act.wait_ge(s_nmax, g + 1)
                    for t in range(TPG):
                        last = nc.scalar.activation(prob[:, c, t, :], lsel[:, c, t, :], ACT.Exp,
                                                    bias=nmax[:, c, t:t + 1], accum_out=psum_p[:, c, t:t + 1])
                    last.then_inc(s_prob, 1)
                if has(i, -1, GROUPS):
                    act.wait_ge(s_x2T_ps, g)
                    nc.scalar.activation(xh[:, bass.ds(GROUP * (g - 1), GROUP)], x2T_ps, ACT.Copy, scale=XS).then_inc(s_xh, 1)
                if has(i, 1, GROUPS):
                    scale_by(k, c, i, range(2, 4))
                if has(i, 0, GROUPS):
                    act.wait_ge(s_prT_ps, g + 1)
                    src = prT_ps.rearrange("p (t n) -> p t n", n=P)
                    nc.scalar.activation(diag[0:NODES, c, :, 0:NODES], src[0:NODES, :, 0:NODES], ACT.Copy)
                    nc.scalar.activation(diag[NODES:P, c, :, NODES:P], src[0:NODES, :, NODES:P], ACT.Copy).then_inc(s_diag, 1)
                if has(i, 1, GROUPS):
                    scale_by(k, c, i, range(4, 5))
                if has(i, -1, GROUPS):
                    act.wait_ge(s_gap, g)
                    nc.scalar.activation(egap[:, o, :], gap[:, :], ACT.Exp, scale=UNSCALE).then_inc(s_egap, 1)

            def scale_by(k, c, i, relations):
                g = 2 * k + c
                for r in relations:
                    if r % 2 == 0 and (i is None or i >= 0):
                        act.wait_ge(s_scores, SB * g + r // 2 + 1)
                    nc.scalar.activation(axT[:, r, :], xnT_ps, ACT.Copy, scale=arel[:, r:r + 1]).then_inc(s_axT, 1)

            act.wait_ge(s_prep, 4)
            pipeline(act, body, GROUPS, 2, 2)

            nc.scalar.preload_act_table(ACT.Gelu)

            def shared(k, c, i):
                u = 2 * k + c
                if i is None or i >= 2:
                    act.wait_ge(s_sh_down, u - 1)
                for f in range(FC):
                    act.wait_ge(s_sh_up, FC * u + f + 1)
                    h = (hid, hid2)[c]
                    nc.scalar.activation(h[:, f, :], bank[:, f, :], ACT.Gelu, bias=b1_f[:, E * FC + f:E * FC + f + 1],
                                         scale=UNSCALE).then_inc(s_sh_hid, 1)

            act.wait_ge(s_scores, SB * GROUPS)
            for i in range(2):
                shared(0, i, i)
            with act.Fori(1, GROUPS // 2) as k:
                shared(k, 0, None)
                shared(k, 1, None)

            act.wait_ge(s_table, 1)

            def body(k, c, i):
                t = 2 * k + c
                if has(i, 0, RTILES):
                    e = expert(act, t, i)
                if has(i, 1, RTILES):
                    act.wait_ge(s_xtT_ps, t + 2)
                    nc.scalar.activation(xth[:, 1 - c, :], bank[:, 6 + (1 - c), 0:RB], ACT.Copy, scale=XS).then_inc(s_xth, 1)
                if has(i, 0, RTILES):
                    if i is None or i >= 2:
                        act.wait_ge(s_down, t - 1)
                    for f in range(FC):
                        if f % 2 == 0:
                            act.wait_ge(s_up, 2 * t + f // 2 + 1)
                        h = (hid, hid2)[c]
                        last = nc.scalar.activation(h[:, f, 0:RB], bank[:, 2 * c + f // 2, RB * (f % 2):RB * (f % 2 + 1)], ACT.Gelu,
                                                    bias=b1_f[:, bass.ds(e * FC + f, 1)], scale=UNSCALE)
                    last.then_inc(s_hid, 1)

            act.wait_ge(s_sh_down, GROUPS)
            pipeline(act, body, RTILES, 1, 0)

            def store(k, c, i):
                g = 2 * k + c
                act.wait_ge(s_add, g + 1)
                act.dma_start(out_v[:, bass.ds(TPG * g, TPG), :], acc[:, bass.ds(TPG * g, TPG), :]).then_inc(s_out, 16)

            with act.Fori(0, GROUPS // 2) as k:
                store(k, 0, None)
                store(k, 1, None)
            act.wait_ge(s_out, 16 * GROUPS)

        @block.vector
        def _(dve):
            V = nc.vector
            dve.wait_ge(s_const, 16 * CONST_DMAS)
            V.tensor_copy(tri[:, :], cst[:, C_TRI:C_TRI + P])
            V.memset(ones[:, :], 1.0)
            V.memset(ones_f[:, :], 1.0)
            V.memset(count[:, 0, :], 0.0)
            V.tensor_copy(place[:, :, :].rearrange("p t k -> p (t k)"), plc[:, K_PLACE:K_PLACE + TPG * TOP])
            V.tensor_scalar(wr_h[:, :], wr_f[:, :], WS, None, ALU.mult).then_inc(s_setup, 1)
            dve.wait_ge(s_setup, 1)
            V.scalar_tensor_tensor(wr_l[:, :], wr_f[:, :], WS, wr_h[:, :], ALU.mult, ALU.subtract).then_inc(s_setup, 1)
            V.tensor_scalar(ang[:, 0, :], cst[0:TIMES, C_REL:C_REL + RELATIONS], tw[:, 0:1], None, ALU.mult).then_inc(s_angle, 1)
            dve.wait_ge(s_angle, 1)
            V.tensor_scalar(ang[:, 1, :], ang[:, 0, :], 1.0 / TWO_PI, MAGIC, ALU.mult, ALU.add).then_inc(s_angle, 1)
            dve.wait_ge(s_angle, 2)
            V.tensor_scalar(ang[:, 2, :], ang[:, 1, :], MAGIC, None, ALU.subtract).then_inc(s_angle, 1)
            dve.wait_ge(s_angle, 3)
            V.scalar_tensor_tensor(ang[:, 0, :], ang[:, 2, :], -PI_HI, ang[:, 0, :], ALU.mult, ALU.add).then_inc(s_angle, 1)
            dve.wait_ge(s_angle, 4)
            V.scalar_tensor_tensor(ang[:, 0, :], ang[:, 2, :], -PI_MID, ang[:, 0, :], ALU.mult, ALU.add).then_inc(s_angle, 1)
            dve.wait_ge(s_angle, 5)
            V.scalar_tensor_tensor(ang[:, 0, :], ang[:, 2, :], -PI_LO, ang[:, 0, :], ALU.mult, ALU.add).then_inc(s_angle, 1)
            dve.wait_ge(s_angle, 6)
            V.scalar_tensor_tensor(ang[:, 1, :], ang[:, 0, :], -1.0, ang[:, 0, :], ALU.mult, ALU.max).then_inc(s_trow, 1)
            dve.wait_ge(s_trow, 1)
            V.tensor_scalar(ang[:, 2, :], ang[:, 1, :], -1.0, HALF_PI, ALU.mult, ALU.add).then_inc(s_angle, 1)
            dve.wait_ge(s_cos, 1)
            V.tensor_tensor(ang[:, 0, :], ang[:, 3, :], trel[:, :], ALU.mult).then_inc(s_tprod, 1)
            dve.wait_ge(s_tsum, 1)
            V.tensor_copy(tsum[:, :], att_ps[:, 0:RELATIONS]).then_inc(s_trow, 1)
            dve.wait_ge(s_trow, 2)
            V.tensor_copy(tparts[:, 0, :], tsum[:, :]).then_inc(s_trow, 1)
            dve.wait_ge(s_trow, 3)
            V.tensor_tensor(trest[:, 0, :], tsum[:, :], tparts[:, 0, :], ALU.subtract).then_inc(s_trow, 1)
            dve.wait_ge(s_trow, 4)
            V.tensor_copy(tparts[:, 1, :], trest[:, 0, :]).then_inc(s_trow, 1)
            dve.wait_ge(s_trow, 5)
            V.tensor_tensor(tparts[:, 2, :], trest[:, 0, :], tparts[:, 1, :], ALU.subtract).then_inc(s_trow, 1)
            dve.wait_ge(s_trow, 6)
            V.tensor_scalar(trow[:, 0, :], tparts[:, 0, :], cst[:, C_PART:C_PART + 1], None, ALU.mult).then_inc(s_trow, 1)
            dve.wait_ge(s_trow, 7)
            V.scalar_tensor_tensor(trow[:, 1, :], tparts[:, 1, :], cst[:, C_PART + 1:C_PART + 2], trow[:, 0, :],
                                   ALU.mult, ALU.add).then_inc(s_trow, 1)
            dve.wait_ge(s_trow, 8)
            V.scalar_tensor_tensor(trow[:, 2, :], tparts[:, 2, :], cst[:, C_PART + 2:C_PART + 3], trow[:, 1, :],
                                   ALU.mult, ALU.add).then_inc(s_trow, 1)
            dve.wait_ge(s_trow, 9)
            V.tensor_copy(time_rows[:, :, :], trow[:, 2, :].unsqueeze(2).to_broadcast([P, RELATIONS, GN])).then_inc(s_time, 1)

            def bn(k, c, i, which, group, done):
                for t in range(TPG):
                    last = V.bn_stats(stats[:, c, which, t, :], acc[:, bass.ds(TPG * group + t, 1), :].rearrange("p a d -> p (a d)"))
                last.then_inc(done, 1)

            def body(k, c, i):
                g = 2 * k + c
                o = 1 - c
                if i == 1:
                    dve.wait_ge(s_w1h, 1)
                    V.scalar_tensor_tensor(w1_l[:, :, :, :].rearrange("p e c f -> p (e c f)"), w1_f[:, :], WS,
                                           w1_h[:, :, :, :].rearrange("p e c f -> p (e c f)"), ALU.mult, ALU.subtract).then_inc(s_w1l, 1)
                if has(i, -2, GROUPS):
                    dve.wait_ge(s_rank, g - 1)
                    V.tensor_tensor(slot[:, :, :], rank_ps, cst[:, C_REGION:C_REGION + E].unsqueeze(1).to_broadcast([P, TPG, E]),
                                    ALU.add).then_inc(s_slot, 1)
                if has(i, -1, GROUPS):
                    dve.wait_ge(s_rstd, g + 2)
                    V.scalar_tensor_tensor(shift2[:, :], mv[:, o, 1, :, 0], -1.0, rstd[:, o, 1, :], ALU.mult, ALU.mult).then_inc(s_shift, 1)
                if has(i, -2, GROUPS):
                    dve.wait_ge(s_slot, g - 1)
                    V.tensor_tensor(slot2[:, :, :, :], onehot[:, c, :, :, :], slot[:, :, :].unsqueeze(2).to_broadcast([P, TPG, TOP, E]),
                                    ALU.mult).then_inc(s_slot2, 1)
                if has(i, 1, GROUPS):
                    dve.wait_ge(s_rstd, g + 2)
                    for t in range(2):
                        first_norm(g, o, t)
                if has(i, -2, GROUPS):
                    dve.wait_ge(s_slot2, g - 1)
                    with nc.allow_low_precision(reason="whole numbers below 2**24, summed in float32"):
                        V.tensor_reduce(pos[:, c, :, :], slot2[:, :, :, :], AX.X, ALU.add).then_inc(s_pos, 1)
                if has(i, 1, GROUPS):
                    first_norm(g, o, 2)
                    first_norm(g, o, 3).then_inc(s_xn, 1)
                    dve.wait_ge(s_adj[o], 16 * (k + c + 1))
                for r in range(RELATIONS):
                    if has(i, 0, GROUPS):
                        if r == 0:
                            hold(dve, s_fill, g + 1)
                        if r % 2 == 0:
                            hold(dve, s_scores, SB * g + r // 2 + 1)
                        if r > 0:
                            hold(dve, s_picked, RELATIONS * g + r)
                        V.copy_predicated(sel[:, c, :, :].rearrange("p t n -> p (t n)"), is_rel[:, c, r, :],
                                          bank[:, r // 2, GN * (r % 2):GN * (r % 2 + 1)]).then_inc(s_picked, 1)
                    if has(i, 1, GROUPS):
                        m = V.tensor_scalar(is_rel[:, o, r, :], adj_sb[:, o, :], float(r + 1), None, ALU.is_equal)
                if has(i, 1, GROUPS):
                    m.then_inc(s_isrel, 1)
                if has(i, 0, GROUPS):
                    dve.wait_ge(s_picked, RELATIONS * (g + 1))
                    V.scalar_tensor_tensor(lsel[:, c, :, :], sel[:, c, :, :], SLOPE, sel[:, c, :, :],
                                           ALU.mult, ALU.max).then_inc(s_lsel, 1)
                if has(i, -1, GROUPS):
                    if i is None or i >= 3:
                        dve.wait_ge(s_sent[o], 16 * TPG * TOP * (k - 1 + c))
                    V.tensor_copy(rowbuf[:, o, :, :, D].bitcast(I32), place[:, :, :]).then_inc(s_ids, 1)
                if has(i, 0, GROUPS):
                    dve.wait_ge(s_lsel, g + 1)
                    V.tensor_reduce(nmax[:, c, :], lsel[:, c, :, :], AX.X, ALU.max, negate=True).then_inc(s_nmax, 1)
                if has(i, -1, GROUPS):
                    dve.wait_ge(s_ids, g)
                    V.tensor_scalar(place[:, :, :], place[:, :, :], float(GROUP), None, ALU.add).then_inc(s_placed, 1)
                if has(i, 2, GROUPS):
                    hold(dve, s_x[c], 16 * (k + 2))
                    bn(k, c, i, 0, g + 2, s_bn1)
                if has(i, -1, GROUPS):
                    dve.wait_ge(s_xh, g)
                    cols = bass.ds(GROUP * (g - 1), GROUP)
                    V.scalar_tensor_tensor(xl[:, cols], x2T_ps, XS, xh[:, cols], ALU.mult, ALU.subtract).then_inc(s_xl, 1)
                if has(i, 2, GROUPS):
                    hold(dve, s_bn1, g + 3)
                    for t in range(TPG):
                        last = V.bn_aggr(mv[:, c, 0, t, :], stats[:, c, 0, t, :])
                    if not has(i, 0, GROUPS):
                        last.then_inc(s_mv, 1)
                if has(i, 0, GROUPS):
                    dve.wait_ge(s_prob, g + 1)
                    V.reciprocal(rsum[:, c, :], psum_p[:, c, :]).then_inc(s_rsum, 1)
                if has(i, -1, GROUPS):
                    dve.wait_ge(s_router, g)
                    V.tensor_copy(logit[:, :, :], router_ps).then_inc(s_logit, 1)
                    hold(dve, s_logit, g)
                    for t in range(TPG):
                        last = V.max(top8[:, t, :], logit[:, t, :])
                    last.then_inc(s_top8, 1)
                if has(i, 0, GROUPS):
                    dve.wait_ge(s_att_ps, g + 1)
                    dve.wait_ge(s_rsum, g + 1)
                    for t in range(TPG):
                        a = acc[:, bass.ds(TPG * g + t, 1), :].rearrange("p a d -> p (a d)")
                        last = V.scalar_tensor_tensor(a, att_ps[:, t * D:(t + 1) * D], rsum[:, c, t:t + 1], a, ALU.mult, ALU.add)
                    last.then_inc(s_after, 1)
                if has(i, -1, GROUPS):
                    dve.wait_ge(s_top8, g)
                    V.tensor_tensor(gap[:, :], top8[:, :, 1], top8[:, :, 0], ALU.subtract).then_inc(s_gap, 1)
                    for t in range(TPG):
                        last = V.max_index(idx8[:, t, :], top8[:, t, :], logit[:, t, :])
                    last.then_inc(s_idx8, 1)
                if has(i, 0, GROUPS):
                    hold(dve, s_after, g + 1)
                    bn(k, c, i, 1, g, s_bn2)
                if has(i, -1, GROUPS):
                    dve.wait_ge(s_idx8, g)
                    V.tensor_copy(idxf[:, :, :], idx8[:, :, 0:TOP]).then_inc(s_idxf, 1)
                if has(i, 0, GROUPS):
                    hold(dve, s_bn2, g + 1)
                    for t in range(TPG):
                        last = V.bn_aggr(mv[:, c, 1, t, :], stats[:, c, 1, t, :])
                    last.then_inc(s_mv, 1)
                if has(i, -1, GROUPS):
                    dve.wait_ge(s_idxf, g)
                    V.tensor_tensor(onehot[:, o, :, :, :], idxf[:, :, :].unsqueeze(3).to_broadcast([P, TPG, TOP, E]),
                                    cst[:, C_IOTA:C_IOTA + E].unsqueeze(1).unsqueeze(1).to_broadcast([P, TPG, TOP, E]),
                                    ALU.is_equal).then_inc(s_onehot, 1)
                    dve.wait_ge(s_egap, g)
                    V.tensor_scalar(e1[:, :], egap[:, o, :], 1.0, None, ALU.add).then_inc(s_e1, 1)
                    dve.wait_ge(s_onehot, g)
                    V.tensor_tensor(chosen[:, o, :, :], onehot[:, o, :, 0, :], onehot[:, o, :, 1, :], ALU.add).then_inc(s_chosen, 1)
                    dve.wait_ge(s_e1, g)
                    V.reciprocal(gates[:, bass.ds(TPG * (g - 1), TPG), 0], e1[:, :]).then_inc(s_gate0, 1)
                    dve.wait_ge(s_chosen, g)
                    V.tensor_reduce(count_g[:, :], chosen[:, o, :, :].rearrange("p t e -> p e t"), AX.X, ALU.add).then_inc(s_count_g, 1)
                    dve.wait_ge(s_gate0, g)
                    V.tensor_tensor(gates[:, bass.ds(TPG * (g - 1), TPG), 1], gates[:, bass.ds(TPG * (g - 1), TPG), 0], egap[:, o, :],
                                    ALU.mult).then_inc(s_gates, 1)
                    dve.wait_ge(s_count_g, g)
                    V.tensor_tensor(count[:, c, :], count[:, o, :], count_g[:, :], ALU.add).then_inc(s_count, 1)

            def first_norm(g, o, t):
                return V.tensor_scalar(xn[:, o, t, :], acc[:, bass.ds(TPG * (g + 1) + t, 1), :].rearrange("p a d -> p (a d)"),
                                       mv[:, o, 0, t, 0:1], rstd[:, o, 0, t:t + 1], ALU.subtract, ALU.mult)

            pipeline(dve, body, GROUPS, 2, 2)

            dve.wait_ge(s_total_ps, 1)
            V.tensor_copy(total[:, :], total_ps).then_inc(s_tab, 1)
            dve.wait_ge(s_tab, 1)
            V.tensor_tensor(first_pad[:, :], total[:, :], cst[:, C_REGION:C_REGION + E], ALU.add)
            V.tensor_scalar(total_i[:, :], total[:, :], float(RB - 1), None, ALU.add).then_inc(s_tab, 1)
            dve.wait_ge(s_tab, 2)
            V.tensor_scalar(n_i[:, :], total_i[:, :], RB.bit_length() - 1, None, ALU.logical_shift_right).then_inc(s_tab, 1)
            dve.wait_ge(s_tab, 3)
            V.tensor_copy(n_f[:, :], n_i[:, :]).then_inc(s_tab, 1)
            prev, done = n_f[:, :], 4
            for step in range(3):
                w = 1 << step
                dve.wait_ge(s_tab, done)
                V.tensor_copy(cum[:, step, 0:w], prev[:, 0:w])
                V.tensor_tensor(cum[:, step, w:E], prev[:, w:E], prev[:, 0:E - w], ALU.add).then_inc(s_tab, 1)
                prev, done = cum[:, step, :], done + 1
            dve.wait_ge(s_tab, 7)
            V.tensor_tensor(past[:, :, :], cst[0:1, C_TILE:C_TILE + RTILES].unsqueeze(2).to_broadcast([1, RTILES, E]),
                            cum[0:1, 2, :].unsqueeze(1).to_broadcast([1, RTILES, E]), ALU.is_ge).then_inc(s_tab, 1)
            dve.wait_ge(s_tab, 8)
            V.tensor_reduce(tile_e[:, :], past[:, :, :], AX.X, ALU.add)
            V.tensor_tensor(past_n[:, :, :], past[:, :, :], n_f[0:1, :].unsqueeze(1).to_broadcast([1, RTILES, E]), ALU.mult).then_inc(s_tab, 1)
            dve.wait_ge(s_tab, 9)
            V.tensor_reduce(tile_b[:, :], past_n[:, :, :], AX.X, ALU.add).then_inc(s_tab, 1)
            dve.wait_ge(s_tab, 10)
            V.tensor_copy(etab[:, :], tile_e[:, :])
            V.tensor_tensor(tile_r[:, :], cst[0:1, C_TILE:C_TILE + RTILES], tile_b[:, :], ALU.subtract).then_inc(s_tab, 1)
            dve.wait_ge(s_tab, 11)
            V.tensor_scalar(tile_b[:, :], tile_e[:, :], float(REGION), None, ALU.mult).then_inc(s_tab, 1)
            dve.wait_ge(s_tab, 12)
            V.scalar_tensor_tensor(rtab[:, :], tile_r[:, :], float(RB), tile_b[:, :], ALU.mult, ALU.add).then_inc(s_table, 1)

            def shared(k, c, i):
                u = 2 * k + c
                a = acc[:, bass.ds(TPG * u, TPG), :]
                V.tensor_tensor(a, a, b2_f[:, E, :].unsqueeze(1).to_broadcast([P, TPG, D]), ALU.add).then_inc(s_sh_bias, 1)
                dve.wait_ge(s_sh_bias, u + 1)
                dve.wait_ge(s_sh_down, u + 1)
                V.tensor_tensor(a, bank[:, 4 + c, :].rearrange("p (t d) -> p t d", d=D), a, ALU.add).then_inc(s_sh_acc, 1)

            with dve.Fori(0, GROUPS // 2) as k:
                shared(k, 0, None)
                shared(k, 1, None)

            def body(k, c, i):
                t = 2 * k + c
                o = 1 - c
                if has(i, -1, RTILES):
                    e = expert(dve, t - 1, i)
                if has(i, 1, RTILES):
                    dve.wait_ge(s_xth, t + 2)
                    V.scalar_tensor_tensor(xtl[:, o, :], bank[:, 6 + o, 0:RB], XS, xth[:, o, :], ALU.mult, ALU.subtract).then_inc(s_xtl, 1)
                if has(i, -1, RTILES):
                    if i is None or i >= 3:
                        dve.wait_ge(s_ysent[o], 16 * RH * (k + c - 1))
                    dve.wait_ge(s_xid, t)
                    V.tensor_copy(yid[:, o, :], xid[:, o, :])
                    dve.wait_ge(s_down, t)
                    V.tensor_tensor(yt[:, o, :, :], bank[:, 4 + o, 0:RH * D].rearrange("p (h d) -> p h d", d=D),
                                    b2_f[:, bass.ds(e, 1), :].to_broadcast([P, RH, D]), ALU.add).then_inc(s_yt, 1)
                if has(i, 1, RTILES):
                    dve.wait_ge(s_xt[o], 16 * (k + c + 1))
                    if i is None or i >= 1:
                        dve.wait_ge(s_yt, t)
                    V.tensor_copy(xid[:, o, :], xt[:, o, :, D].bitcast(I32)).then_inc(s_xid, 1)

            pipeline(dve, body, RTILES, 1, 1)

            def combine(k, c, i):
                g = 2 * k + c
                dve.wait_ge(s_yb[c], 32 * (k + 1))
                for j in range(TOP):
                    for t in range(TPG):
                        a = acc[:, bass.ds(TPG * g + t, 1), :].rearrange("p a d -> p (a d)")
                        last = V.scalar_tensor_tensor(a, yb[:, c, j, t, :], gates[:, bass.ds(TPG * g + t, 1), j], a, ALU.mult, ALU.add)
                    last.then_inc((s_add0, s_add)[j], 1)
                    if j == 0:
                        dve.wait_ge(s_add0, g + 1)

            with dve.Fori(0, GROUPS // 2) as k:
                combine(k, 0, None)
                combine(k, 1, None)

        @block.tensor
        def _(pe):
            MM = nc.tensor.matmul
            pe.wait_ge(s_setup, 2)
            pe.wait_ge(s_tprod, 1)
            MM(att_ps[:, 0:RELATIONS], ones_f[:, :], ang[:, 0, :], start=True, stop=True).then_inc(s_tsum, 1)
            pe.wait_ge(s_time, 1)

            def scores(k, c, i, banks):
                g = 2 * k + c + 1
                for q in banks:
                    rels = range(2 * q, min(2 * q + 2, RELATIONS))
                    w = len(rels) * GN
                    pe.wait_ge(s_axT, RELATIONS * g + rels[-1] + 1)
                    if i is None or i >= 0:
                        pe.wait_ge(s_picked, RELATIONS * (g - 1) + rels[-1] + 1)
                    for n in range(2 * TPG):
                        half = slice(n % 2 * NODES, (n % 2 + 1) * NODES)
                        out_ps = bank[half, q, 0:w].rearrange("p (r t n) -> p r t n", t=TPG, n=NODES)[:, :, n // 2, :]
                        MM(out_ps, xnT[:, 1 - c, n * NODES:(n + 1) * NODES],
                           axT[:, rels[0]:rels[-1] + 1, n * NODES:(n + 1) * NODES], start=(n < 2), stop=False, skip_group_check=True)
                    MM(bank[:, q, 0:w], ones[:, :], time_rows[:, rels[0]:rels[-1] + 1, :].rearrange("p r n -> p (r n)"),
                       start=False, stop=True, skip_group_check=True).then_inc(s_scores, 1)

            def body(k, c, i):
                g = 2 * k + c
                o = 1 - c
                if has(i, -2, GROUPS):
                    pe.wait_ge(s_count, g - 1)
                    MM(rank_ps, tri[:, :], chosen[:, c, :, :], start=True, stop=False)
                    for t in range(TPG - 1):
                        MM(rank_ps[:, t + 1:TPG, :], ones[:, :], chosen[:, c, t:t + 1, :].to_broadcast([P, TPG - 1 - t, E]), start=False, stop=False)
                    MM(rank_ps, ones[:, :], count[:, c:c + 1, :].to_broadcast([P, TPG, E]), start=False, stop=True).then_inc(s_rank, 1)
                if has(i, 1, GROUPS):
                    pe.wait_ge(s_xn, g + 2)
                    for t in range(TPG):
                        last = nc.tensor.transpose(xnT_ps[:, t * P:(t + 1) * P], xn[:, o, t, :], ident)
                    last.then_inc(s_xnT_ps, 1)
                if has(i, -1, GROUPS):
                    pe.wait_ge(s_xn2, g)
                    for t in range(TPG):
                        last = nc.tensor.transpose(x2T_ps[:, t * P:(t + 1) * P], rowbuf[:, o, t, 0, 0:D], ident)
                    last.then_inc(s_x2T_ps, 1)
                if has(i, 1, GROUPS):
                    scores(k, c, i, range(0, 1))
                if has(i, 0, GROUPS):
                    hold(pe, s_prob, g + 1)
                    for t in range(TPG):
                        last = nc.tensor.transpose(prT_ps[0:NODES, t * P:(t + 1) * P], prob[:, c, t, :], ident)
                    last.then_inc(s_prT_ps, 1)
                if has(i, -1, GROUPS):
                    pe.wait_ge(s_xl, g)
                    if i is None or i >= 2:
                        pe.wait_ge(s_slot, g - 1)
                    for t in range(TPG):
                        cols = bass.ds(GROUP * (g - 1) + t * P, P)
                        MM(router_ps[:, t, :], xh[:, cols], wr_h[:, :], start=True, stop=False)
                        MM(router_ps[:, t, :], xh[:, cols], wr_l[:, :], start=False, stop=False)
                        last = MM(router_ps[:, t, :], xl[:, cols], wr_h[:, :], start=False, stop=True)
                    last.then_inc(s_router, 1)
                if has(i, 0, GROUPS):
                    pe.wait_ge(s_diag, g + 1)
                    for t in range(TPG):
                        last = MM(att_ps[:, t * D:(t + 1) * D], diag[:, c, t, :], xn[:, c, t, :], start=True, stop=True)
                    last.then_inc(s_att_ps, 1)
                if has(i, 1, GROUPS):
                    scores(k, c, i, range(1, SB))

            pipeline(pe, body, GROUPS, 2, 2)

            pe.wait_ge(s_count, GROUPS)
            pe.wait_ge(s_pos, GROUPS)
            MM(total_ps, ones[:, :], count[:, GROUPS % 2, :], start=True, stop=True).then_inc(s_total_ps, 1)
            pe.wait_ge(s_w1l, 1)

            def up(k, c, i):
                u = 2 * k + c
                for f in range(FC):
                    if i != 0:
                        pe.wait_ge(s_sh_hid, FC * (u - 1) + f + 1)
                    xs = (xh[:, bass.ds(GROUP * u, GROUP)], xl[:, bass.ds(GROUP * u, GROUP)])
                    MM(bank[:, f, :], w1_h[:, E, f, :], xs[0], start=True, stop=False)
                    MM(bank[:, f, :], w1_h[:, E, f, :], xs[1], start=False, stop=False)
                    MM(bank[:, f, :], w1_l[:, E, f, :], xs[0], start=False, stop=True).then_inc(s_sh_up, 1)

            def down(k, c, i):
                u = 2 * k + c
                pe.wait_ge(s_sh_hid, FC * (u + 1))
                if i is None or i >= 2:
                    pe.wait_ge(s_sh_acc, u - 1)
                for t in range(TPG):
                    for f in range(FC):
                        last = MM(bank[:, 4 + c, t * D:(t + 1) * D], (hid, hid2)[c][:, f, t * P:(t + 1) * P], w2_f[:, E, f, :],
                                  start=(f == 0), stop=(f == FC - 1))
                last.then_inc(s_sh_down, 1)

            up(0, 0, 0)
            up(0, 1, 1)
            down(0, 0, 0)
            with pe.Fori(1, GROUPS // 2) as k:
                up(k, 0, None)
                down(k - 1, 1, 2)
                up(k, 1, None)
                down(k, 0, None)
            down(GROUPS // 2 - 1, 1, GROUPS - 1)
            pe.wait_ge(s_sh_acc, GROUPS)

            def body(k, c, i):
                t = 2 * k + c
                o = 1 - c
                if has(i, 0, RTILES):
                    e = expert(pe, t, i)
                if has(i, -1, RTILES):
                    e_last = expert(pe, t - 1, i)
                if has(i, 1, RTILES):
                    pe.wait_ge(s_xt[o], 16 * (k + c + 1))
                    for h in range(RH):
                        last = nc.tensor.transpose(bank[:, 6 + o, h * P:(h + 1) * P], xt[:, o, h, 0:D], ident)
                    last.then_inc(s_xtT_ps, 1)
                if has(i, 0, RTILES):
                    pe.wait_ge(s_xtl, t + 1)
                    for f in range(FC):
                        ps = bank[:, 2 * c + f // 2, RB * (f % 2):RB * (f % 2 + 1)]
                        wh = w1_h[:, bass.ds(e, 1), f, :].rearrange("p a f -> p (a f)")
                        wl = w1_l[:, bass.ds(e, 1), f, :].rearrange("p a f -> p (a f)")
                        MM(ps, wh, xth[:, c, :], start=True, stop=False)
                        MM(ps, wh, xtl[:, c, :], start=False, stop=False)
                        last = MM(ps, wl, xth[:, c, :], start=False, stop=True)
                        if f % 2:
                            last.then_inc(s_up, 1)
                        if f == 2 and (i is None or i >= 3):
                            pe.wait_ge(s_yt, t - 2)
                if has(i, -1, RTILES):
                    if i == RTILES:
                        pe.wait_ge(s_yt, t - 2)
                    pe.wait_ge(s_hid, t)
                    for h in range(RH):
                        for f in range(FC):
                            last = MM(bank[:, 4 + o, h * D:(h + 1) * D], (hid, hid2)[o][:, f, h * P:(h + 1) * P],
                                      w2_f[:, bass.ds(e_last, 1), f, :].rearrange("p a d -> p (a d)"), start=(f == 0), stop=(f == FC - 1))
                    last.then_inc(s_down, 1)

            pe.wait_ge(s_table, 1)
            pipeline(pe, body, RTILES, 1, 1)


def kernel(**inputs):
    import numpy as np
    from concourse import bacc
    from concourse.bass_utils import run_bass_kernel_spmd

    g = {name.replace("L0_gnn_", "").replace("L0_ffn_", ""): np.asarray(a) for name, a in inputs.items()}
    p = np.arange(P)
    constants = np.zeros((P, C_ALL), np.float32)
    constants[:, C_IDENT:C_IDENT + P] = np.eye(P)
    constants[:, C_TRI:C_TRI + P] = p[:, None] < p[None, :]
    constants[:, C_IOTA:C_IOTA + E] = np.arange(E)
    constants[:, C_REGION:C_REGION + E] = np.arange(E) * REGION
    constants[:, C_PART:C_PART + 3] = np.eye(P)[:, 0:3]
    constants[:, C_REL:C_REL + RELATIONS] = np.arange(1, RELATIONS + 1)
    constants[:, C_TILE:C_TILE + RTILES] = np.arange(RTILES)
    places = np.zeros((P, K_ALL), np.int32)
    t, k = np.meshgrid(np.arange(TPG), np.arange(TOP), indexing="ij")
    places[:, K_PLACE:K_PLACE + TPG * TOP] = p[:, None] + (t * P + k * TOKENS).reshape(1, -1)
    places[:, K_PAD:K_PAD + E * RH] = TOP * TOKENS + p[:, None] + P * np.arange(E * RH)
    places[:, K_SPARE:K_SPARE + E * RH] = TOP * TOKENS + E * RB + p[:, None] + P * np.arange(E * RH)

    def chunks(b):
        return np.ascontiguousarray(b.reshape(-1, P).T)

    arrays = {
        "x": g["x"].reshape(TOKENS, D),
        "adj": g["adj"].reshape(TOKENS, NODES),
        "a_relT": np.ascontiguousarray(g["a_rel"].T),
        "t_relT": np.ascontiguousarray(g["t_rel"].T),
        "time_w": g["time_w"].reshape(TIMES, 1),
        "wr": g["Wr"],
        "w1": np.concatenate([g["W1p"], g["W1s"][None]]),
        "w2": np.concatenate([g["W2p"], g["W2s"][None]]),
        "b1T": chunks(np.concatenate([g["b1p"].reshape(-1), g["b1s"]])),
        "b2": np.ascontiguousarray(np.broadcast_to(np.concatenate([g["b2p"].reshape(-1), g["b2s"]]), (P, (E + 1) * D))),
        "constants": constants,
        "places": places,
    }
    nc = bacc.Bacc("TRN2", target_bir_lowering=False, num_devices=1)
    args = [nc.dram_tensor(n, a.shape, mybir.dt.from_np(a.dtype), kind="ExternalInput").ap() for n, a in arrays.items()]
    out = nc.dram_tensor("out", (TOKENS, D), F32, kind="ExternalOutput").ap()
    rows = nc.dram_tensor("expert_rows", (ROWS, RW), F32, kind="Internal").ap()
    results = nc.dram_tensor("expert_results", (YROWS, D), F32, kind="Internal").ap()
    build(nc, *args, out, rows, results)
    r = run_bass_kernel_spmd(nc, [arrays], core_ids=[0])
    return r.results[0]["out"].reshape(GRAPHS, NODES, D)
```

```python
from contextlib import ExitStack

import concourse.bass as bass
from concourse import mybir

F32 = mybir.dt.float32
F16 = mybir.dt.float16
BF16 = mybir.dt.bfloat16
I32 = mybir.dt.int32
U32 = mybir.dt.uint32
ALU = mybir.AluOpType
ACT = mybir.ActivationFunctionType
AX = mybir.AxisListType

P = 128
GRAPHS, NODES, D = 128, 64, 128
TOKENS = GRAPHS * NODES
RELATIONS = 5
TIMES = 64
E = 8
F = 512
FC = F // P
TOP = 2
TPG = 4
GROUP = TPG * P
GROUPS = TOKENS // GROUP
TILES = TOKENS // P
GN = TPG * NODES
SB = (RELATIONS + 1) // 2
RB = 256
RH = RB // P
REGION = TOKENS + RB
RTILES = TOP * TOKENS // RB + E
CT = 8
STEPS = TILES // CT
HALF = GROUPS // 4
ROWS = E * REGION + E * RB
RW = D + 2
YROWS = TOP * TOKENS + 2 * E * RB
EPS = 1e-5
NEG = -9000000000000000.0
SLOPE = 0.2
XS = 2.0 ** 6
WS = 2.0 ** 8
HS = 2.0 ** 4
UNSCALE = 1.0 / (XS * WS)
UNSCALE2 = 1.0 / (HS * WS)
BS = 2.0 ** 6
TWO_PI = 6.283185307179586
PI_HI = 6.28125
PI_MID = 0.0019350051879882812
PI_LO = 3.0199159819597e-07
HALF_PI = TWO_PI / 4
MAGIC = 12582912.0

C_IDENT, C_TRI, C_IOTA, C_REGION, C_PART, C_REL, C_TILE = 0, P, 2 * P, 2 * P + E, 2 * P + 2 * E, 2 * P + 2 * E + 3, 2 * P + 2 * E + 3 + RELATIONS
C_ROW = C_TILE + RTILES
C_ALL = C_ROW + 1
K_PLACE, K_PAD, K_SPARE = 0, 2 * TPG * TOP, 2 * TPG * TOP + E * RH
K_ALL = K_SPARE + E * RH


def build(nc, x, adj, a_relT, t_relT, time_w, wr, w1, w2, b1, b1T, b2, b2s, constants, places, out, rows_dram, results_dram):
    x_v = x.rearrange("(t p) d -> p t d", p=P)
    adj_v = adj.rearrange("(t p) n -> p t n", p=P)
    out_v = out.rearrange("(t p) d -> p t d", p=P)
    results_v = results_dram[0:TOP * TOKENS, :].rearrange("(k t p) d -> p k t d", p=P, k=TOP)

    with ExitStack() as ctx:
        def sb(name, shape, dt):
            return ctx.enter_context(nc.sbuf_tensor(name, shape, dt))

        def sem(name):
            return ctx.enter_context(nc.semaphore(name))

        cst = sb("cst", [P, C_ALL], F32)
        plc = sb("plc", [P, K_ALL], I32)
        ident = cst[:, C_IDENT:C_IDENT + P]
        arel = sb("arel", [P, RELATIONS], F32)
        wr_f = sb("wr_f", [P, E], F32)
        wr_h = sb("wr_h", [P, E], F16)
        wr_l = sb("wr_l", [P, E], F16)
        w_f = sb("w_f", [P, (E + 1) * F], F32)
        w1_h = sb("w1_h", [P, E + 1, FC, P], F16)
        w1_l = sb("w1_l", [P, E + 1, FC, P], F16)
        w2_h = sb("w2_h", [P, E + 1, FC, D], F16)
        w2_l = sb("w2_l", [P, E + 1, FC, D], F16)
        b1_f = sb("b1_f", [P, (E + 1) * FC], F32)
        b1_rows = sb("b1_rows", [E + 1, F], F32)
        b2_in = sb("b2_in", [E + 1, D], F32)
        b2_f = sb("b2_f", [P, D], F32)
        xn = sb("xn", [P, 2, TPG, D], F32)
        b2_rows = sb("b2_rows", [P, D], F16)
        b2_ones = sb("b2_ones", [P, P], F16)
        tri = sb("tri", [P, P], BF16)
        ones = sb("ones", [P, P], BF16)
        ones_f = sb("ones_f", [TIMES, P], F32)
        minus_half = sb("minus_half", [P, 2, TPG], F32)
        tw = sb("tw", [TIMES, 1], F32)
        trel = sb("trel", [TIMES, RELATIONS], F32)
        ang = sb("ang", [TIMES, 4, RELATIONS], F32)
        tsum = sb("tsum", [P, RELATIONS], F32)
        tparts = sb("tparts", [P, 3, RELATIONS], BF16)
        trest = sb("trest", [P, 2, RELATIONS], F32)
        trow = sb("trow", [P, 3, RELATIONS], F32)
        time_rows = sb("time_rows", [P, RELATIONS, GN], BF16)
        acc = sb("acc", [P, TILES, D], F32)
        xh = sb("xh", [P, TOKENS], F16)
        xl = sb("xl", [P, TOKENS], F16)
        adj_sb = sb("adj_sb", [P, 2, TPG * NODES], I32)
        is_rel = sb("is_rel", [P, 2, RELATIONS, TPG * NODES], I32)
        stats = sb("stats", [P, 2, 2, TPG, 6], F32)
        mv = sb("mv", [P, 2, 2, TPG, 2], F32)
        var_eps = sb("var_eps", [P, 2, 2, TPG], F32)
        rstd = sb("rstd", [P, 2, 2, TPG], F32)
        shift2 = sb("shift2", [P, TPG], F32)
        xnT = sb("xnT", [P, 2, GROUP], F32)
        axT = sb("axT", [P, RELATIONS, GROUP], F32)
        sel = sb("sel", [P, 2, TPG, NODES], F32)
        lsel = sb("lsel", [P, 2, TPG, NODES], F32)
        nmax = sb("nmax", [P, 2, TPG], F32)
        prob = sb("prob", [P, 2, TPG, NODES], F32)
        psum_p = sb("psum_p", [P, 2, TPG], F32)
        rsum = sb("rsum", [P, 2, TPG], F32)
        diag = sb("diag", [P, 2, TPG, P], F32)
        rowbuf = sb("rowbuf", [P, 2, TPG, TOP, RW], F32)
        top8 = sb("top8", [P, TPG, E], F32)
        idx8 = sb("idx8", [P, TPG, E], U32)
        idxf = sb("idxf", [P, TPG, TOP], F32)
        onehot = sb("onehot", [P, 2, TPG, TOP, E], F32)
        chosen = sb("chosen", [P, 2, TPG, E], BF16)
        count_g = sb("count_g", [P, E], F32)
        count = sb("count", [P, 3, E], BF16)
        gap = sb("gap", [P, TPG], F32)
        egap = sb("egap", [P, 2, TPG], F32)
        e1 = sb("e1", [P, TPG], F32)
        slot = sb("slot", [P, TPG, E], F32)
        slot2 = sb("slot2", [P, TPG, TOP, E], F32)
        pos = sb("pos", [P, 2, TPG, TOP], I32)
        total = sb("total", [P, E], F32)
        total_i = sb("total_i", [P, E], I32)
        first_pad = sb("first_pad", [P, E], I32)
        n_i = sb("n_i", [P, E], I32)
        n_f = sb("n_f", [P, E], F32)
        cum = sb("cum", [P, 3, E], F32)
        past, past_n = (a.rearrange("p a b -> p (a b)")[0:E + 1, 0:RTILES * E].rearrange("p (t e) -> p t e", e=E)
                        for a in (xnT[:, :, :], diag[:, :, :, :].rearrange("p c t n -> p c (t n)")))
        tile_e = sb("tile_e", [E + 1, RTILES], F32)
        is_expert = sb("is_expert", [E + 1, RTILES], F32)
        tile_b = sb("tile_b", [1, RTILES], F32)
        tile_r = sb("tile_r", [1, RTILES], F32)
        etab = sb("etab", [1, RTILES], I32)
        rtab = sb("rtab", [1, RTILES], I32)
        padrows = sb("padrows", [P, E * RH, RW], F32)
        hid = axT[:, 0:FC, :]
        hid_parts = sb("hid_parts", [P, 2, FC, GROUP], F16)
        b2_h = hid_parts[:, :, :, :].rearrange("p w f n -> p (w f n)")[:, 0:D]
        hid_parts2 = is_rel[:, :, :, :].rearrange("p c r n -> p (c r n)")[:, 0:FC * GROUP].bitcast(F16).rearrange(
            "p (w f n) -> p w f n", w=2, f=FC)
        parts = (hid_parts[:, :, :, :], hid_parts2)
        xt = sb("xt", [P, 2, RH, RW], F32)
        bias_t = sb("bias_t", [P, FC + 1, RTILES], F32)
        xth = sb("xth", [P, 2, RB], F16)
        xtl = sb("xtl", [P, 2, RB], F16)
        yT = sb("yT", [P, 2, RB], F32)
        yt = xn[:, :, 0:RH, :]
        xtail = sb("xtail", [P, RTILES, RH, 2], F32)
        yid = sb("yid", [P, 2, RH], I32)
        yb = w_f[:, 0:2 * TOP * CT * D].rearrange("p (c k t d) -> p c k t d", c=2, k=TOP, t=CT)

        bank = ctx.enter_context(nc.psum_tensor("bank", [P, 8, 512], F32))

        xnT_ps, x2T_ps, prT_ps, att_ps = (bank[:, b, :] for b in (3, 4, 5, 6))
        router_ps = bank[:, 7, 0:TPG * E].rearrange("p (t e) -> p t e", e=E)
        rank_ps = bank[:, 7, 64:64 + TPG * E].rearrange("p (t e) -> p t e", e=E)
        total_ps = bank[:, 7, 128:128 + E]

        s_first = sem("s_first")
        s_const = sem("s_const")
        s_w1 = sem("s_w1")
        s_x = [sem("s_x_even"), sem("s_x_odd")]
        s_adj = [sem("s_adj0"), sem("s_adj1")]
        s_held = sem("s_held")
        s_b2 = sem("s_b2")
        s_setup = sem("s_setup")
        s_angle = sem("s_angle")
        s_cos = sem("s_cos")
        s_tprod = sem("s_tprod")
        s_tsum = sem("s_tsum")
        s_trow = sem("s_trow")
        s_time = sem("s_time")
        s_prep = sem("s_prep")
        s_w1h = sem("s_w1h")
        s_w1l = sem("s_w1l")
        s_w2 = sem("s_w2")
        s_w2h = sem("s_w2h")
        s_w2l = sem("s_w2l")
        s_bn = sem("s_bn")
        s_mv = sem("s_mv")
        s_var = sem("s_var")
        s_rstd = sem("s_rstd")
        s_shift = sem("s_shift")
        s_xn = sem("s_xn")
        s_isrel = sem("s_isrel")
        s_xnT_ps = sem("s_xnT_ps")
        s_xnT = sem("s_xnT")
        s_axT = sem("s_axT")
        s_fill = sem("s_fill")
        s_scores = sem("s_scores")
        s_picked = sem("s_picked")
        s_lsel = sem("s_lsel")
        s_nmax = sem("s_nmax")
        s_prob = sem("s_prob")
        s_prT_ps = sem("s_prT_ps")
        s_diag = sem("s_diag")
        s_rsum = sem("s_rsum")
        s_att_ps = sem("s_att_ps")
        s_after = sem("s_after")
        s_xn2 = sem("s_xn2")
        s_x2T_ps = sem("s_x2T_ps")
        s_xh = sem("s_xh")
        s_xl = sem("s_xl")
        s_router = sem("s_router")
        s_top8 = sem("s_top8")
        s_idx8 = sem("s_idx8")
        s_idxf = sem("s_idxf")
        s_onehot = sem("s_onehot")
        s_chosen = sem("s_chosen")
        s_count_g = sem("s_count_g")
        s_count = sem("s_count")
        s_gap = sem("s_gap")
        s_egap = sem("s_egap")
        s_e1 = sem("s_e1")
        s_gate0 = sem("s_gate0")
        s_gates = sem("s_gates")
        s_rank = sem("s_rank")
        s_slot = sem("s_slot")
        s_slot2 = sem("s_slot2")
        s_pos = sem("s_pos")
        s_sent = [sem("s_sent0"), sem("s_sent1")]
        s_spare = sem("s_spare")
        s_padids = sem("s_padids")
        s_padded = sem("s_padded")
        s_total_ps = sem("s_total_ps")
        s_tab = sem("s_tab")
        s_table = sem("s_table")
        s_bias = sem("s_bias")
        s_bias_t = sem("s_bias_t")
        s_sh_up = sem("s_sh_up")
        s_sh_hid = sem("s_sh_hid")
        s_sh_high = sem("s_sh_high")
        s_sh_low = sem("s_sh_low")
        s_sh_down = sem("s_sh_down")
        s_sh_acc = sem("s_sh_acc")
        s_xt = [sem("s_xt0"), sem("s_xt1")]
        s_xtT_ps = sem("s_xtT_ps")
        s_xth = sem("s_xth")
        s_xtl = sem("s_xtl")
        s_up = sem("s_up")
        s_hid = sem("s_hid")
        s_high = sem("s_high")
        s_low = sem("s_low")
        s_down = sem("s_down")
        s_yT = sem("s_yT")
        s_back = sem("s_back")
        s_xtail = sem("s_xtail")
        s_yt = sem("s_yt")
        s_ysent = [sem("s_ysent0"), sem("s_ysent1")]
        s_yb = [sem("s_yb0"), sem("s_yb1")]
        s_add0 = sem("s_add0")
        s_add = sem("s_add")
        s_out = sem("s_out")

        CONST_DMAS = 7
        block = ctx.enter_context(nc.Block())

        def pipeline(engine, body, n, before, after, pairs=1):
            end = 2 + ((n - 2) // 2 - 2) // pairs * pairs
            for i in range(-before, 4):
                body(i // 2, i % 2, i)
            with engine.Fori(2, end - pairs + 1, pairs) as k:
                for pair in range(pairs):
                    body(k + pair, 0, None)
                    body(k + pair, 1, None)
            for i in range(2 * end, n + after):
                body(i // 2, i % 2, i)

        def hold(engine, semaphore, value):
            engine.wait_ge(semaphore, value)
            engine.sem_inc(s_held, 1)

        def expert(engine, t, i):
            col = etab[0:1, bass.ds(t, 1)] if i is None else etab[0:1, t:t + 1]
            return engine.value_load(col, min_val=0, max_val=E)

        def at(part, k, c, i, d, *more):
            if has(i, d, GROUPS):
                return part(k + (c + d) // 2, (c + d) % 2, None if i is None else i + d, *more)

        def has(i, d, n):
            return i is None or 0 <= i + d < n

        @block.sync
        def _(sp):
            def load_x(k, c, i):
                g = 2 * k + c
                if i is None or i >= 2:
                    hold(sp, s_x[c], 16 * k)
                sp.dma_start(acc[:, bass.ds(TPG * g, TPG), :], x_v[:, bass.ds(TPG * g, TPG), :]).then_inc(s_x[c], 16)

            def load_adj(k, c, i):
                g = 2 * k + c
                if i is None or i >= 2:
                    hold(sp, s_adj[c], 16 * k)
                    hold(sp, s_isrel, g - 1)
                sp.dma_start(adj_sb[:, c, :].rearrange("p (t n) -> p t n", n=NODES),
                             adj_v[:, bass.ds(TPG * g, TPG), :]).then_inc(s_adj[c], 16)

            load_x(0, 0, 0)
            sp.dma_start(cst[:, :], constants).then_inc(s_first, 16)
            sp.dma_start(tw[:, :], time_w).then_inc(s_first, 16)
            sp.dma_start(trel[:, :], t_relT).then_inc(s_first, 16)
            load_adj(0, 0, 0)
            load_x(0, 1, 1)
            load_adj(0, 1, 1)
            sp.dma_start(plc[:, :], places).then_inc(s_const, 16)
            sp.dma_start(arel[:, :], a_relT).then_inc(s_const, 16)
            sp.dma_start(wr_f[:, :], wr).then_inc(s_const, 16)
            sp.dma_start(b1_rows[:, :], b1).then_inc(s_const, 16)
            sp.dma_start(b1_f[:, :], b1T).then_inc(s_const, 16)
            sp.dma_start(b2_in[:, :], b2).then_inc(s_const, 16)
            sp.dma_start(b2_f[:, :], b2s).then_inc(s_const, 16)

            load_x(1, 0, 2)
            load_x(1, 1, 3)
            sp.dma_start(w_f[:, :].rearrange("p (e f) -> p e f", e=E + 1), w1.rearrange("e d f -> d e f")).then_inc(s_w1, 16)
            load_adj(1, 0, 2)
            load_adj(1, 1, 3)
            with sp.Fori(2, GROUPS // 2) as k:
                for c in range(2):
                    load_x(k, c, None)
                    load_adj(k, c, None)

            sp.wait_ge(s_w1l, 3)
            sp.dma_start(w_f[:, :].rearrange("p (e c d) -> p (e c) d", e=E + 1, c=FC),
                         w2.rearrange("e (c p) d -> p (e c) d", p=P)).then_inc(s_w2, 16)

            sp.wait_ge(s_table, 1)
            sp.wait_ge(s_padids, 2)
            for e in range(E):
                row = sp.value_load(first_pad[0:1, e:e + 1], min_val=0, max_val=ROWS - RB)
                sp.dma_start(rows_dram[bass.ds(row, RB), :].rearrange("(h p) w -> p h w", p=P),
                             padrows[:, RH * e:RH * (e + 1), :]).then_inc(s_padded, 16)

            for c in range(2):
                sp.wait_ge(s_sent[c], 16 * TPG * TOP * GROUPS // 2)
            sp.wait_ge(s_spare, 16)
            sp.wait_ge(s_padded, 16 * E)

            def load_tile(k, c, i):
                t = 2 * k + c
                col = rtab[0:1, bass.ds(t, 1)] if i is None else rtab[0:1, t:t + 1]
                row = sp.value_load(col, min_val=0, max_val=ROWS - RB)
                if i is None or i >= 2:
                    hold(sp, s_xt[c], 16 * k)
                    hold(sp, s_xtail, t - 1)
                    hold(sp, s_xtT_ps, t - 1)
                sp.dma_start(xt[:, c, :, :], rows_dram[bass.ds(row, RB), :].rearrange("(h p) w -> p h w", p=P)).then_inc(s_xt[c], 16)

            for i in range(2):
                load_tile(0, i, i)
            with sp.Fori(1, RTILES // 2) as k:
                load_tile(k, 0, None)
                load_tile(k, 1, None)

            for c in range(2):
                sp.wait_ge(s_ysent[c], 16 * RH * RTILES // 2)

            def load_results(k, c, i):
                m = 2 * k + c
                if i is None or i >= 2:
                    hold(sp, s_yb[c], 32 * k)
                for j in range(TOP):
                    sp.dma_start(yb[:, c, j, :, :], results_v[:, j, bass.ds(CT * m, CT), :]).then_inc(s_yb[c], 16)

            def store(k, c):
                m = 2 * k + c
                sp.wait_ge(s_add, m + 1)
                sp.dma_start(out_v[:, bass.ds(CT * m, CT), :], acc[:, bass.ds(CT * m, CT), :]).then_inc(s_out, 16)

            for i in range(2):
                load_results(0, i, i)
            with sp.Fori(1, STEPS // 2) as k:
                for c in range(2):
                    store(k - 1, c)
                    load_results(k, c, None)
            for c in range(2):
                store(STEPS // 2 - 1, c)
            sp.wait_ge(s_out, 16 * STEPS)

        @block.gpsimd
        def _(pool):
            nc.gpsimd.memset(padrows[:, :, :], 0.0).then_inc(s_prep, 1)
            nc.gpsimd.memset(diag[:, :, :, :], 0.0).then_inc(s_prep, 1)
            nc.gpsimd.memset(minus_half[:, :, :], -0.5).then_inc(s_prep, 1)
            def fill(k, c, i):
                if i is None or i >= 2:
                    hold(pool, s_lsel, 2 * k + c - 1)
                nc.gpsimd.memset(sel[:, c, :, :], NEG).then_inc(s_fill, 1)

            def scatter(k, c, i):
                hold(pool, s_pos, 2 * k + c + 1)
                for t in range(TPG):
                    for j in range(TOP):
                        nc.gpsimd.indirect_dma_start(
                            out=rows_dram[:, :], out_offset=bass.IndirectOffsetOnAxis(ap=pos[:, c, t, j:j + 1], axis=0),
                            in_=rowbuf[:, c, t, j, :], in_offset=None).then_inc(s_sent[c], 16)

            def deviations(k, c, i):
                g = 2 * k + c
                if has(i, -1, GROUPS) or has(i, 2, GROUPS):
                    w = slice(0 if has(i, 2, GROUPS) else 1, 2 if has(i, -1, GROUPS) else 1)
                    hold(pool, s_mv, g + 3)
                    nc.gpsimd.tensor_scalar(var_eps[:, c, w, :], mv[:, c, w, :, 1], EPS, None, ALU.add).then_inc(s_var, 1)
                    pool.wait_ge(s_var, g + 3)
                    nc.gpsimd.tensor_tensor(rstd[:, c, w, :], var_eps[:, c, w, :], minus_half[:, w, :], ALU.pow).then_inc(s_rstd, 1)

            pool.wait_ge(s_prep, 3)
            deviations(-1, 0, -2)
            pool.wait_ge(s_const, 16 * CONST_DMAS)
            nc.gpsimd.tensor_copy(padrows[:, :, D:D + 1].bitcast(I32),
                                  plc[:, K_SPARE:K_SPARE + E * RH].rearrange("p (r o) -> p r o", o=1)).then_inc(s_padids, 1)
            pool.wait_ge(s_padids, 1)
            pool.dma_start(rows_dram[E * REGION:ROWS, :].rearrange("(r p) w -> p r w", p=P), padrows[:, :, :]).then_inc(s_spare, 16)

            def body(k, c, i):
                at(fill, k, c, i, 1)
                at(scatter, k, c, i, -3)
                deviations(k, c, i)

            pipeline(pool, body, GROUPS, 1, 3)

            pool.wait_ge(s_spare, 16)
            nc.gpsimd.tensor_copy(padrows[:, :, D:D + 1].bitcast(I32),
                                  plc[:, K_PAD:K_PAD + E * RH].rearrange("p (r o) -> p r o", o=1)).then_inc(s_padids, 1)

            def send_results(k, c, i):
                t = 2 * k + c
                hold(pool, s_yt, t + 1)
                for h in range(RH):
                    nc.gpsimd.indirect_dma_start(
                        out=results_dram[:, :], out_offset=bass.IndirectOffsetOnAxis(ap=yid[:, c, h:h + 1], axis=0),
                        in_=yt[:, c, h, :], in_offset=None).then_inc(s_ysent[c], 16)

            with pool.Fori(0, RTILES // 2) as k:
                send_results(k, 0, None)
                send_results(k, 1, None)

        @block.scalar
        def _(act):
            act.wait_ge(s_angle, 7)
            nc.scalar.activation(ang[:, 3, :], ang[:, 2, :], ACT.Sin).then_inc(s_cos, 1)
            nc.scalar.preload_act_table(ACT.Exp)

            def second_norm(k, c, i):
                g = 2 * k + c
                act.wait_ge(s_shift, g + 1)
                if i is None or i >= 2:
                    act.wait_ge(s_sent[c], 16 * TPG * TOP * k)
                for t in range(TPG):
                    last = nc.scalar.activation(rowbuf[:, c, t, :, 0:D], acc[:, bass.ds(TPG * g + t, 1), :].to_broadcast([P, TOP, D]),
                                                ACT.Identity, bias=shift2[:, t:t + 1], scale=rstd[:, 1 - c, 1, t:t + 1])
                last.then_inc(s_xn2, 1)

            def first_normT(k, c, i):
                act.wait_ge(s_xnT_ps, 2 * k + c + 1)
                nc.scalar.activation(xnT[:, c, :], xnT_ps, ACT.Copy).then_inc(s_xnT, 1)

            def scale_by(k, c, i, relations):
                g = 2 * k + c
                for r in relations:
                    if r % 2 == 0 and (i is None or i >= 1):
                        act.wait_ge(s_scores, SB * (g - 1) + r // 2 + 1)
                    nc.scalar.activation(axT[:, r, :], xnT_ps, ACT.Copy, scale=arel[:, r:r + 1]).then_inc(s_axT, 1)

            def exponentials(k, c, i):
                act.wait_ge(s_nmax, 2 * k + c + 1)
                for t in range(TPG):
                    last = nc.scalar.activation(prob[:, c, t, :], lsel[:, c, t, :], ACT.Exp,
                                                bias=nmax[:, c, t:t + 1], accum_out=psum_p[:, c, t:t + 1])
                last.then_inc(s_prob, 1)

            def high_part(k, c, i):
                g = 2 * k + c
                act.wait_ge(s_x2T_ps, g + 1)
                nc.scalar.activation(xh[:, bass.ds(GROUP * g, GROUP)], x2T_ps, ACT.Copy, scale=XS).then_inc(s_xh, 1)

            def to_diagonal(k, c, i):
                act.wait_ge(s_prT_ps, 2 * k + c + 1)
                src = prT_ps.rearrange("p (t n) -> p t n", n=P)
                nc.scalar.activation(diag[0:NODES, c, :, 0:NODES], src[0:NODES, :, 0:NODES], ACT.Copy)
                nc.scalar.activation(diag[NODES:P, c, :, NODES:P], src[0:NODES, :, NODES:P], ACT.Copy).then_inc(s_diag, 1)

            def gate_exp(k, c, i):
                act.wait_ge(s_gap, 2 * k + c + 1)
                nc.scalar.activation(egap[:, c, :], gap[:, :], ACT.Exp, scale=UNSCALE).then_inc(s_egap, 1)

            def body(k, c, i):
                if i in range(0, 3):
                    act.wait_ge(s_w1, 16)
                    nc.scalar.activation(w1_h[:, 3 * i:3 * i + 3, :, :].rearrange("p e c f -> p (e c f)"), w_f[:, 3 * i * F:3 * (i + 1) * F],
                                         ACT.Copy, scale=WS).then_inc(s_w1h, 1)
                if i == GROUPS:
                    act.wait_ge(s_w2, 16)
                    nc.scalar.activation(w2_h[:, :, :, :].rearrange("p e c d -> p (e c d)"), w_f[:, :], ACT.Copy, scale=WS).then_inc(s_w2h, 1)
                at(gate_exp, k, c, i, -3)
                at(to_diagonal, k, c, i, -1)
                at(scale_by, k, c, i, 0, range(4, 5))
                at(second_norm, k, c, i, -2)
                at(first_normT, k, c, i, 1)
                at(scale_by, k, c, i, 1, range(0, 1))
                at(scale_by, k, c, i, 1, range(1, 2))
                at(high_part, k, c, i, -2)
                at(scale_by, k, c, i, 1, range(2, 3))
                at(exponentials, k, c, i, 0)
                at(scale_by, k, c, i, 1, range(3, 4))
            act.wait_ge(s_prep, 3)
            act.wait_ge(s_const, 16 * CONST_DMAS)
            pipeline(act, body, GROUPS, 2, 3)

            nc.scalar.preload_act_table(ACT.Gelu)

            def shared(k, c, i):
                u = 2 * k + c
                for f in range(FC):
                    if i is None or i >= 1:
                        act.wait_ge(s_sh_low, 2 * (u - 1) + f // 2 + 1)
                    act.wait_ge(s_sh_up, FC * u + f + 1)
                    nc.scalar.activation(hid[:, f, :], bank[:, f, :], ACT.Gelu, bias=b1_f[:, E * FC + f:E * FC + f + 1],
                                         scale=UNSCALE).then_inc(s_sh_hid, 1)
                    if f % 2:
                        if f == 1 and (i is None or i >= 2):
                            act.wait_ge(s_sh_down, u - 1)
                        act.wait_ge(s_sh_hid, FC * u + f + 1)
                        nc.scalar.activation(parts[c][:, 0, f - 1:f + 1, :], hid[:, f - 1:f + 1, :], ACT.Copy, scale=HS).then_inc(s_sh_high, 1)

            act.wait_ge(s_scores, SB * GROUPS)
            act.wait_ge(s_picked, RELATIONS * GROUPS)
            for i in range(2):
                shared(0, i, i)
            with act.Fori(1, HALF) as k:
                shared(k, 0, None)
                shared(k, 1, None)

            act.wait_ge(s_bias_t, 1)

            def body(k, c, i):
                t = 2 * k + c
                for f in range(FC if has(i, 0, RTILES) else 0):
                    if f % 2 == 0:
                        if i is None or i >= 2:
                            act.wait_ge(s_low, 2 * (t - 2) + f // 2 + 1)
                        act.wait_ge(s_up, 2 * t + f // 2 + 1)
                    last = nc.scalar.activation(hid[:, f, RB * c:RB * (c + 1)], bank[:, 2 * c + f // 2, RB * (f % 2):RB * (f % 2 + 1)],
                                                ACT.Gelu, bias=bias_t[:, f, bass.ds(t, 1)], scale=UNSCALE)
                    if f % 2:
                        last.then_inc(s_hid, 1)
                        if f == 1 and (i is None or i >= 2):
                            act.wait_ge(s_down, t - 1)
                        act.wait_ge(s_hid, 2 * t + f // 2 + 1)
                        nc.scalar.activation(parts[c][:, 0, f - 1:f + 1, 0:RB], hid[:, f - 1:f + 1, RB * c:RB * (c + 1)],
                                             ACT.Copy, scale=HS).then_inc(s_high, 1)
                if has(i, -1, RTILES):
                    o = 1 - c
                    if i is None or i >= 3:
                        act.wait_ge(s_back, t - 2)
                    act.wait_ge(s_down, t)
                    nc.scalar.activation(yT[:, o, :], bank[:, 4 + o, 0:RB], ACT.Identity, bias=bias_t[:, FC, bass.ds(t - 1, 1)],
                                         scale=UNSCALE2).then_inc(s_yT, 1)

            act.wait_ge(s_sh_down, 2 * HALF)
            pipeline(act, body, RTILES, 0, 1)

            act.wait_ge(s_low, 2 * RTILES)
            act.wait_ge(s_down, RTILES)
            with act.Fori(HALF, 2 * HALF) as k:
                shared(k, 0, None)
                shared(k, 1, None)

        @block.vector
        def _(dve):
            V = nc.vector
            def bn(c, which, group):
                for t in range(TPG):
                    last = V.bn_stats(stats[:, c, which, t, :], acc[:, bass.ds(TPG * group + t, 1), :].rearrange("p a d -> p (a d)"))
                return last

            def statistics(k, c, i):
                g = 2 * k + c
                last = None
                if has(i, 2, GROUPS):
                    hold(dve, s_x[c], 16 * (k + 2))
                    last = bn(c, 0, g + 2)
                if has(i, -1, GROUPS):
                    hold(dve, s_after, g)
                    last = bn(c, 1, g - 1)
                if last is not None:
                    last.then_inc(s_bn, 1)
                    hold(dve, s_bn, g + 3)
                    for which, d in enumerate((2, -1)):
                        if has(i, d, GROUPS):
                            for t in range(TPG):
                                last = V.bn_aggr(mv[:, c, which, t, :], stats[:, c, which, t, :])
                    last.then_inc(s_mv, 1)

            statistics(-1, 0, -2)
            V.memset(ones_f[:, :], 1.0)
            V.memset(ones[:, :], 1.0)
            dve.wait_ge(s_first, 48)
            V.tensor_scalar(ang[:, 0, :], cst[0:TIMES, C_REL:C_REL + RELATIONS], tw[:, 0:1], None, ALU.mult).then_inc(s_angle, 1)
            dve.wait_ge(s_angle, 1)
            V.tensor_scalar(ang[:, 1, :], ang[:, 0, :], 1.0 / TWO_PI, MAGIC, ALU.mult, ALU.add).then_inc(s_angle, 1)
            dve.wait_ge(s_angle, 2)
            V.tensor_scalar(ang[:, 2, :], ang[:, 1, :], MAGIC, None, ALU.subtract).then_inc(s_angle, 1)
            dve.wait_ge(s_angle, 3)
            V.scalar_tensor_tensor(ang[:, 0, :], ang[:, 2, :], -PI_HI, ang[:, 0, :], ALU.mult, ALU.add).then_inc(s_angle, 1)
            dve.wait_ge(s_angle, 4)
            V.scalar_tensor_tensor(ang[:, 0, :], ang[:, 2, :], -PI_MID, ang[:, 0, :], ALU.mult, ALU.add).then_inc(s_angle, 1)
            dve.wait_ge(s_angle, 5)
            V.scalar_tensor_tensor(ang[:, 0, :], ang[:, 2, :], -PI_LO, ang[:, 0, :], ALU.mult, ALU.add).then_inc(s_angle, 1)
            dve.wait_ge(s_angle, 6)
            V.scalar_tensor_tensor(ang[:, 1, :], ang[:, 0, :], -1.0, ang[:, 0, :], ALU.mult, ALU.max).then_inc(s_trow, 1)
            dve.wait_ge(s_trow, 1)
            V.tensor_scalar(ang[:, 2, :], ang[:, 1, :], -1.0, HALF_PI, ALU.mult, ALU.add).then_inc(s_angle, 1)
            dve.wait_ge(s_cos, 1)
            V.tensor_tensor(ang[:, 0, :], ang[:, 3, :], trel[:, :], ALU.mult).then_inc(s_tprod, 1)
            dve.wait_ge(s_tsum, 1)
            V.tensor_copy(tsum[:, :], att_ps[:, 0:RELATIONS]).then_inc(s_trow, 1)
            dve.wait_ge(s_trow, 2)
            V.tensor_copy(tparts[:, 0, :], tsum[:, :]).then_inc(s_trow, 1)
            dve.wait_ge(s_trow, 3)
            V.tensor_tensor(trest[:, 0, :], tsum[:, :], tparts[:, 0, :], ALU.subtract).then_inc(s_trow, 1)
            dve.wait_ge(s_trow, 4)
            V.tensor_copy(tparts[:, 1, :], trest[:, 0, :]).then_inc(s_trow, 1)
            dve.wait_ge(s_trow, 5)
            V.tensor_tensor(tparts[:, 2, :], trest[:, 0, :], tparts[:, 1, :], ALU.subtract).then_inc(s_trow, 1)
            dve.wait_ge(s_trow, 6)
            V.tensor_scalar(trow[:, 0, :], tparts[:, 0, :], cst[:, C_PART:C_PART + 1], None, ALU.mult).then_inc(s_trow, 1)
            dve.wait_ge(s_trow, 7)
            V.scalar_tensor_tensor(trow[:, 1, :], tparts[:, 1, :], cst[:, C_PART + 1:C_PART + 2], trow[:, 0, :],
                                   ALU.mult, ALU.add).then_inc(s_trow, 1)
            dve.wait_ge(s_trow, 8)
            V.scalar_tensor_tensor(trow[:, 2, :], tparts[:, 2, :], cst[:, C_PART + 2:C_PART + 3], trow[:, 1, :],
                                   ALU.mult, ALU.add).then_inc(s_trow, 1)
            dve.wait_ge(s_trow, 9)
            V.tensor_copy(time_rows[:, :, :], trow[:, 2, :].unsqueeze(2).to_broadcast([P, RELATIONS, GN])).then_inc(s_time, 1)

            dve.wait_ge(s_const, 16 * CONST_DMAS)
            V.tensor_copy(tri[:, :], cst[:, C_TRI:C_TRI + P])
            V.memset(count[:, 0, :], 0.0)
            V.tensor_copy(rowbuf[:, :, :, :, D].bitcast(I32),
                          plc[:, K_PLACE:K_PLACE + 2 * TPG * TOP].rearrange("p (c t k) -> p c t k", c=2, k=TOP))
            V.tensor_scalar(wr_h[:, :], wr_f[:, :], WS, None, ALU.mult).then_inc(s_setup, 1)
            dve.wait_ge(s_setup, 1)
            V.scalar_tensor_tensor(wr_l[:, :], wr_f[:, :], WS, wr_h[:, :], ALU.mult, ALU.subtract).then_inc(s_setup, 1)
            def bias_rows():
                V.memset(b2_ones[:, :], HS * WS / BS)
                V.tensor_scalar(b2_h[:, :], b2_f[:, :], BS, None, ALU.mult).then_inc(s_b2, 1)
                dve.wait_ge(s_b2, 1)
                V.scalar_tensor_tensor(b2_rows[:, :], b2_f[:, :], BS, b2_h[:, :], ALU.mult, ALU.subtract).then_inc(s_b2, 1)
                dve.wait_ge(s_b2, 2)
                V.tensor_scalar(b2_rows[:, :], b2_rows[:, :], cst[:, C_PART + 1:C_PART + 2], None, ALU.mult).then_inc(s_b2, 1)
                dve.wait_ge(s_b2, 3)
                V.scalar_tensor_tensor(b2_rows[:, :], b2_h[:, :], cst[:, C_PART:C_PART + 1], b2_rows[:, :],
                                       ALU.mult, ALU.add).then_inc(s_b2, 1)

            def first_norm(k, c, i):
                g = 2 * k + c
                dve.wait_ge(s_rstd, g + 1)
                if i is None or i >= 2:
                    dve.wait_ge(s_att_ps, g - 1)
                for t in range(TPG):
                    last = V.tensor_scalar(xn[:, c, t, :], acc[:, bass.ds(TPG * g + t, 1), :].rearrange("p a d -> p (a d)"),
                                           mv[:, c, 0, t, 0:1], rstd[:, c, 0, t:t + 1], ALU.subtract, ALU.mult)
                last.then_inc(s_xn, 1)

            def mask(k, c, i, r):
                if r == 0:
                    dve.wait_ge(s_adj[c], 16 * (k + 1))
                m = V.tensor_scalar(is_rel[:, c, r, :], adj_sb[:, c, :], float(r + 1), None, ALU.is_equal)
                if r == RELATIONS - 1:
                    m.then_inc(s_isrel, 1)

            def pick(k, c, i, r):
                g = 2 * k + c
                if r == 0:
                    hold(dve, s_fill, g + 1)
                if r % 2 == 0:
                    hold(dve, s_scores, SB * g + r // 2 + 1)
                if r > 0:
                    hold(dve, s_picked, RELATIONS * g + r)
                V.copy_predicated(sel[:, c, :, :].rearrange("p t n -> p (t n)"), is_rel[:, c, r, :],
                                  bank[:, r // 2, GN * (r % 2):GN * (r % 2 + 1)]).then_inc(s_picked, 1)

            def leaky(k, c, i):
                g = 2 * k + c
                dve.wait_ge(s_picked, RELATIONS * (g + 1))
                V.scalar_tensor_tensor(lsel[:, c, :, :], sel[:, c, :, :], SLOPE, sel[:, c, :, :],
                                       ALU.mult, ALU.max).then_inc(s_lsel, 1)

            def maximum(k, c, i):
                dve.wait_ge(s_lsel, 2 * k + c + 1)
                V.tensor_reduce(nmax[:, c, :], lsel[:, c, :, :], AX.X, ALU.max, negate=True).then_inc(s_nmax, 1)

            def sums(k, c, i):
                dve.wait_ge(s_prob, 2 * k + c + 1)
                V.reciprocal(rsum[:, c, :], psum_p[:, c, :]).then_inc(s_rsum, 1)

            def after(k, c, i):
                g = 2 * k + c
                dve.wait_ge(s_att_ps, g + 1)
                dve.wait_ge(s_rsum, g + 1)
                for t in range(TPG):
                    a = acc[:, bass.ds(TPG * g + t, 1), :].rearrange("p a d -> p (a d)")
                    last = V.scalar_tensor_tensor(a, att_ps[:, t * D:(t + 1) * D], rsum[:, c, t:t + 1], a, ALU.mult, ALU.add)
                last.then_inc(s_after, 1)

            def shift(k, c, i):
                g = 2 * k + c
                dve.wait_ge(s_rstd, g + 4)
                V.scalar_tensor_tensor(shift2[:, :], mv[:, 1 - c, 1, :, 0], -1.0, rstd[:, 1 - c, 1, :], ALU.mult, ALU.mult).then_inc(s_shift, 1)

            def low_part(k, c, i):
                g = 2 * k + c
                dve.wait_ge(s_xh, g + 1)
                cols = bass.ds(GROUP * g, GROUP)
                V.scalar_tensor_tensor(xl[:, cols], x2T_ps, XS, xh[:, cols], ALU.mult, ALU.subtract).then_inc(s_xl, 1)

            def result_places(k, c, i):
                if i is None or i >= 2:
                    dve.wait_ge(s_sent[c], 16 * TPG * TOP * k)
                ids = rowbuf[:, c, :, :, D].bitcast(I32)
                V.tensor_scalar(ids, ids, float(2 * GROUP), None, ALU.add)

            def top_two(k, c, i, part):
                g = 2 * k + c
                if part == 0:
                    hold(dve, s_router, g + 1)
                    for t in range(TPG):
                        last = V.max(top8[:, t, :], router_ps[:, t, :])
                    last.then_inc(s_top8, 1)
                if part == 1:
                    dve.wait_ge(s_top8, g + 1)
                    V.tensor_tensor(gap[:, :], top8[:, :, 1], top8[:, :, 0], ALU.subtract).then_inc(s_gap, 1)
                    for t in range(TPG):
                        last = V.max_index(idx8[:, t, :], top8[:, t, :], router_ps[:, t, :])
                    last.then_inc(s_idx8, 1)

            def choices(k, c, i, part):
                g = 2 * k + c
                o = 1 - c
                if part == 0:
                    dve.wait_ge(s_idx8, g + 1)
                    V.tensor_copy(idxf[:, :, :], idx8[:, :, 0:TOP]).then_inc(s_idxf, 1)
                if part == 1:
                    dve.wait_ge(s_idxf, g + 1)
                    V.tensor_tensor(onehot[:, c, :, :, :], idxf[:, :, :].unsqueeze(3).to_broadcast([P, TPG, TOP, E]),
                                    cst[:, C_IOTA:C_IOTA + E].unsqueeze(1).unsqueeze(1).to_broadcast([P, TPG, TOP, E]),
                                    ALU.is_equal).then_inc(s_onehot, 1)
                if part == 2:
                    dve.wait_ge(s_onehot, g + 1)
                    V.tensor_tensor(chosen[:, c, :, :], onehot[:, c, :, 0, :], onehot[:, c, :, 1, :], ALU.add).then_inc(s_chosen, 1)
                if part == 3:
                    dve.wait_ge(s_chosen, g + 1)
                    V.tensor_reduce(count_g[:, :], chosen[:, c, :, :].rearrange("p t e -> p e t"), AX.X, ALU.add).then_inc(s_count_g, 1)
                if part == 4:
                    dve.wait_ge(s_count_g, g + 1)
                    V.tensor_tensor(count[:, o, :], count[:, c, :], count_g[:, :], ALU.add).then_inc(s_count, 1)

            def gates(k, c, i, part):
                g = 2 * k + c
                if part == 0:
                    dve.wait_ge(s_egap, g + 1)
                    V.tensor_scalar(e1[:, :], egap[:, c, :], 1.0, None, ALU.add).then_inc(s_e1, 1)
                if part == 1:
                    dve.wait_ge(s_e1, g + 1)
                    V.reciprocal(rowbuf[:, c, :, 0, D + 1], e1[:, :]).then_inc(s_gate0, 1)
                if part == 2:
                    dve.wait_ge(s_gate0, g + 1)
                    V.tensor_tensor(rowbuf[:, c, :, 1, D + 1], rowbuf[:, c, :, 0, D + 1], egap[:, c, :], ALU.mult).then_inc(s_gates, 1)

            def place_in_region(k, c, i, part):
                g = 2 * k + c
                if part == 0:
                    dve.wait_ge(s_rank, g + 1)
                    V.tensor_tensor(slot[:, :, :], rank_ps, cst[:, C_REGION:C_REGION + E].unsqueeze(1).to_broadcast([P, TPG, E]),
                                    ALU.add).then_inc(s_slot, 1)
                if part == 1:
                    dve.wait_ge(s_slot, g + 1)
                    V.tensor_tensor(slot2[:, :, :, :], onehot[:, c, :, :, :], slot[:, :, :].unsqueeze(2).to_broadcast([P, TPG, TOP, E]),
                                    ALU.mult).then_inc(s_slot2, 1)
                if part == 2:
                    dve.wait_ge(s_slot2, g + 1)
                    with nc.allow_low_precision(reason="whole numbers below 2**24, summed in float32"):
                        V.tensor_reduce(pos[:, c, :, :], slot2[:, :, :, :], AX.X, ALU.add).then_inc(s_pos, 1)

            def second_low(first, end):
                dve.wait_ge(s_w2h, 1)
                low, high = (w[:, first:end, :, :].rearrange("p e c d -> p (e c d)") for w in (w2_l, w2_h))
                V.scalar_tensor_tensor(low, w_f[:, first * F:end * F], WS, high, ALU.mult, ALU.subtract).then_inc(s_w2l, 1)

            def body(k, c, i):
                if i == 0:
                    bias_rows()
                if i in range(1, 4):
                    dve.wait_ge(s_w1h, i)
                    V.scalar_tensor_tensor(w1_l[:, 3 * i - 3:3 * i, :, :].rearrange("p e c f -> p (e c f)"), w_f[:, 3 * (i - 1) * F:3 * i * F], WS,
                                           w1_h[:, 3 * i - 3:3 * i, :, :].rearrange("p e c f -> p (e c f)"), ALU.mult, ALU.subtract).then_inc(s_w1l, 1)
                if i == GROUPS + 1:
                    second_low(E, E + 1)
                at(mask, k, c, i, 1, 0)
                at(pick, k, c, i, 0, 0)
                at(place_in_region, k, c, i, -3, 0)
                at(mask, k, c, i, 1, 1)
                at(gates, k, c, i, -3, 2)
                at(shift, k, c, i, -2)
                at(place_in_region, k, c, i, -3, 1)
                at(pick, k, c, i, 0, 1)
                at(place_in_region, k, c, i, -3, 2)
                at(first_norm, k, c, i, 1)
                at(pick, k, c, i, 0, 2)
                at(mask, k, c, i, 1, 2)
                at(pick, k, c, i, 0, 3)
                at(mask, k, c, i, 1, 3)
                at(pick, k, c, i, 0, 4)
                at(sums, k, c, i, -1)
                at(leaky, k, c, i, 0)
                at(maximum, k, c, i, 0)
                at(after, k, c, i, -1)
                at(low_part, k, c, i, -2)
                statistics(k, c, i)
                at(top_two, k, c, i, -2, 0)
                at(result_places, k, c, i, -2)
                at(top_two, k, c, i, -2, 1)
                at(choices, k, c, i, -2, 0)
                at(mask, k, c, i, 1, 4)
                at(choices, k, c, i, -2, 1)
                at(choices, k, c, i, -2, 2)
                at(gates, k, c, i, -2, 0)
                at(choices, k, c, i, -2, 3)
                at(choices, k, c, i, -2, 4)
                at(gates, k, c, i, -2, 1)

            pipeline(dve, body, GROUPS, 1, 3)

            def shared_low(k, c, i):
                u = 2 * k + c
                for j in range(FC // 2):
                    dve.wait_ge(s_sh_high, 2 * u + j + 1)
                    V.scalar_tensor_tensor(parts[c][:, 1, 2 * j:2 * j + 2, :], hid[:, 2 * j:2 * j + 2, :], HS, parts[c][:, 0, 2 * j:2 * j + 2, :],
                                           ALU.mult, ALU.subtract).then_inc(s_sh_low, 1)

            def shared(k, c, i):
                u = 2 * k + c
                a = acc[:, bass.ds(TPG * u, TPG), :]
                dve.wait_ge(s_sh_down, u + 1)
                V.scalar_tensor_tensor(a, bank[:, 4 + c, :].rearrange("p (t d) -> p t d", d=D), UNSCALE2, a, ALU.mult, ALU.add).then_inc(s_sh_acc, 1)

            dve.wait_ge(s_total_ps, 1)
            V.tensor_copy(total[:, :], total_ps).then_inc(s_tab, 1)
            dve.wait_ge(s_tab, 1)
            V.tensor_tensor(first_pad[:, :], total[:, :], cst[:, C_REGION:C_REGION + E], ALU.add)
            V.tensor_scalar(total_i[:, :], total[:, :], float(RB - 1), None, ALU.add).then_inc(s_tab, 1)
            dve.wait_ge(s_tab, 2)
            V.tensor_scalar(n_i[:, :], total_i[:, :], RB.bit_length() - 1, None, ALU.logical_shift_right).then_inc(s_tab, 1)
            dve.wait_ge(s_tab, 3)
            V.tensor_copy(n_f[:, :], n_i[:, :]).then_inc(s_tab, 1)
            prev, done = n_f[:, :], 4
            for step in range(3):
                w = 1 << step
                dve.wait_ge(s_tab, done)
                V.tensor_copy(cum[:, step, 0:w], prev[:, 0:w])
                V.tensor_tensor(cum[:, step, w:E], prev[:, w:E], prev[:, 0:E - w], ALU.add).then_inc(s_tab, 1)
                prev, done = cum[:, step, :], done + 1
            shared_low(0, 0, 0)
            dve.wait_ge(s_tab, 7)
            V.tensor_tensor(past[:, :, :], cst[0:E + 1, C_TILE:C_TILE + RTILES].unsqueeze(2).to_broadcast([E + 1, RTILES, E]),
                            cum[0:E + 1, 2, :].unsqueeze(1).to_broadcast([E + 1, RTILES, E]), ALU.is_ge).then_inc(s_tab, 1)
            dve.wait_ge(s_tab, 8)
            V.tensor_reduce(tile_e[:, :], past[:, :, :], AX.X, ALU.add)
            V.tensor_tensor(past_n[:, :, :], past[:, :, :], n_f[0:E + 1, :].unsqueeze(1).to_broadcast([E + 1, RTILES, E]), ALU.mult).then_inc(s_tab, 1)
            dve.wait_ge(s_tab, 9)
            V.tensor_reduce(tile_b[:, :], past_n[0:1, :, :], AX.X, ALU.add).then_inc(s_tab, 1)
            dve.wait_ge(s_tab, 10)
            V.tensor_scalar(is_expert[:, :], tile_e[:, :], cst[0:E + 1, C_ROW:C_ROW + 1], None, ALU.is_equal)
            V.tensor_copy(etab[:, :], tile_e[0:1, :])
            V.tensor_tensor(tile_r[:, :], cst[0:1, C_TILE:C_TILE + RTILES], tile_b[:, :], ALU.subtract).then_inc(s_tab, 1)
            dve.wait_ge(s_tab, 11)
            V.tensor_scalar(tile_b[:, :], tile_e[0:1, :], float(REGION), None, ALU.mult).then_inc(s_tab, 1)
            dve.wait_ge(s_tab, 12)
            V.scalar_tensor_tensor(rtab[:, :], tile_r[:, :], float(RB), tile_b[:, :], ALU.mult, ALU.add).then_inc(s_table, 1)

            second_low(0, E // 2)
            shared_low(0, 1, 1)
            shared(0, 0, 0)
            dve.wait_ge(s_bias, 1)
            V.tensor_copy(bias_t[:, :, :], bank[:, 6, 0:(FC + 1) * RTILES].rearrange("p (f t) -> p f t", t=RTILES)).then_inc(s_bias_t, 1)
            second_low(E // 2, E)
            with dve.Fori(1, HALF) as k:
                shared_low(k, 0, None)
                shared(k - 1, 1, None)
                shared_low(k, 1, None)
                shared(k, 0, None)
            shared(HALF - 1, 1, None)

            def hidden_low(t, c, j):
                dve.wait_ge(s_high, 2 * t + j + 1)
                V.scalar_tensor_tensor(parts[c][:, 1, 2 * j:2 * j + 2, 0:RB], hid[:, 2 * j:2 * j + 2, RB * c:RB * (c + 1)], HS,
                                       parts[c][:, 0, 2 * j:2 * j + 2, 0:RB], ALU.mult, ALU.subtract).then_inc(s_low, 1)

            def body(k, c, i):
                t = 2 * k + c
                o = 1 - c
                if has(i, 1, RTILES):
                    dve.wait_ge(s_xt[o], 16 * (k + c + 1))
                    V.tensor_copy(xtail[:, bass.ds(t + 1, 1), :, :].rearrange("p a h w -> p (a h) w"), xt[:, o, :, D:RW]).then_inc(s_xtail, 1)
                    dve.wait_ge(s_xtT_ps, t + 2)
                    V.tensor_scalar(xth[:, o, :], bank[:, 6 + o, 0:RB], XS, None, ALU.mult).then_inc(s_xth, 1)
                    dve.wait_ge(s_xth, t + 2)
                    V.scalar_tensor_tensor(xtl[:, o, :], bank[:, 6 + o, 0:RB], XS, xth[:, o, :], ALU.mult, ALU.subtract).then_inc(s_xtl, 1)
                if has(i, 0, RTILES):
                    hidden_low(t, c, 0)
                if has(i, -2, RTILES):
                    if i is None or i >= 4:
                        dve.wait_ge(s_ysent[c], 16 * RH * (k - 1))
                    dve.wait_ge(s_xtail, t - 1)
                    tail = xtail[:, bass.ds(t - 2, 1), :, :].rearrange("p a h w -> p (a h) w")
                    V.tensor_copy(yid[:, c, :], tail[:, :, 0].bitcast(I32))
                    dve.wait_ge(s_back, t - 1)
                    V.tensor_tensor(yt[:, c, :, :], bank[:, 4 + c, RB:2 * RB].rearrange("p (h d) -> p h d", d=D),
                                    tail[:, :, 1:2].to_broadcast([P, RH, D]), ALU.mult).then_inc(s_yt, 1)
                if has(i, 0, RTILES):
                    hidden_low(t, c, 1)

            pipeline(dve, body, RTILES, 1, 2)

            def combine(k, c, i):
                m = 2 * k + c
                dve.wait_ge(s_yb[c], 32 * (k + 1))
                dve.wait_ge(s_sh_acc, CT // TPG * (m + 1))
                a = acc[:, bass.ds(CT * m, CT), :]
                V.tensor_tensor(a, a, yb[:, c, 0, :, :], ALU.add).then_inc(s_add0, 1)
                dve.wait_ge(s_add0, m + 1)
                V.tensor_tensor(a, a, yb[:, c, 1, :, :], ALU.add).then_inc(s_add, 1)

            shared_low(HALF, 0, None)
            shared_low(HALF, 1, None)
            shared(HALF, 0, None)
            combine(0, 0, 0)
            with dve.Fori(HALF + 1, 2 * HALF) as k:
                shared_low(k, 0, None)
                shared(k - 1, 1, None)
                combine(k - HALF - 1, 1, None)
                shared_low(k, 1, None)
                shared(k, 0, None)
                combine(k - HALF, 0, None)
            shared(2 * HALF - 1, 1, None)
            combine(HALF - 1, 1, None)

        @block.tensor
        def _(pe):
            MM = nc.tensor.matmul
            pe.wait_ge(s_tprod, 1)
            MM(att_ps[:, 0:RELATIONS], ones_f[:, :], ang[:, 0, :], start=True, stop=True).then_inc(s_tsum, 1)
            pe.wait_ge(s_time, 1)

            def scores(k, c, i, banks):
                g = 2 * k + c
                for q in banks:
                    rels = range(2 * q, min(2 * q + 2, RELATIONS))
                    w = len(rels) * GN
                    pe.wait_ge(s_axT, RELATIONS * g + rels[-1] + 1)
                    if i is None or i >= 1:
                        pe.wait_ge(s_picked, RELATIONS * (g - 1) + rels[-1] + 1)
                    for n in range(2 * TPG):
                        half = slice(n % 2 * NODES, (n % 2 + 1) * NODES)
                        out_ps = bank[half, q, 0:w].rearrange("p (r t n) -> p r t n", t=TPG, n=NODES)[:, :, n // 2, :]
                        MM(out_ps, xnT[:, c, n * NODES:(n + 1) * NODES],
                           axT[:, rels[0]:rels[-1] + 1, n * NODES:(n + 1) * NODES], start=(n < 2), stop=False, skip_group_check=True)
                    MM(bank[:, q, 0:w], ones[:, :], time_rows[:, rels[0]:rels[-1] + 1, :].rearrange("p r n -> p (r n)"),
                       start=False, stop=True, skip_group_check=True).then_inc(s_scores, 1)

            def ranks(k, c, i):
                pe.wait_ge(s_count, 2 * k + c + 1)
                MM(rank_ps, tri[:, :], chosen[:, c, :, :], start=True, stop=False)
                for t in range(TPG - 1):
                    MM(rank_ps[:, t + 1:TPG, :], ones[:, :], chosen[:, c, t:t + 1, :].to_broadcast([P, TPG - 1 - t, E]), start=False, stop=False)
                MM(rank_ps, ones[:, :], count[:, c:c + 1, :].to_broadcast([P, TPG, E]), start=False, stop=True).then_inc(s_rank, 1)

            def transpose_first(k, c, i):
                pe.wait_ge(s_xn, 2 * k + c + 1)
                if i is None or i >= 1:
                    pe.wait_ge(s_axT, RELATIONS * (2 * k + c))
                for t in range(TPG):
                    last = nc.tensor.transpose(xnT_ps[:, t * P:(t + 1) * P], xn[:, c, t, :], ident)
                last.then_inc(s_xnT_ps, 1)

            def transpose_second(k, c, i):
                pe.wait_ge(s_xn2, 2 * k + c + 1)
                for t in range(TPG):
                    last = nc.tensor.transpose(x2T_ps[:, t * P:(t + 1) * P], rowbuf[:, c, t, 0, 0:D], ident)
                last.then_inc(s_x2T_ps, 1)

            def transpose_prob(k, c, i):
                hold(pe, s_prob, 2 * k + c + 1)
                for t in range(TPG):
                    last = nc.tensor.transpose(prT_ps[0:NODES, t * P:(t + 1) * P], prob[:, c, t, :], ident)
                last.then_inc(s_prT_ps, 1)

            def router(k, c, i):
                g = 2 * k + c
                pe.wait_ge(s_xl, g + 1)
                if i is None or i >= 1:
                    pe.wait_ge(s_slot, g)
                for t in range(TPG):
                    cols = bass.ds(GROUP * g + t * P, P)
                    MM(router_ps[:, t, :], xh[:, cols], wr_h[:, :], start=True, stop=False)
                    MM(router_ps[:, t, :], xh[:, cols], wr_l[:, :], start=False, stop=False)
                    last = MM(router_ps[:, t, :], xl[:, cols], wr_h[:, :], start=False, stop=True)
                last.then_inc(s_router, 1)

            def attend(k, c, i):
                g = 2 * k + c
                pe.wait_ge(s_diag, g + 1)
                if i is None or i >= 1:
                    pe.wait_ge(s_after, g)
                for t in range(TPG):
                    last = MM(att_ps[:, t * D:(t + 1) * D], diag[:, c, t, :], xn[:, c, t, :], start=True, stop=True)
                last.then_inc(s_att_ps, 1)

            def up(k, c, i):
                u = 2 * k + c
                for f in range(FC):
                    if i != 0:
                        pe.wait_ge(s_sh_hid, FC * (u - 1) + f + 1)
                    xs = (xh[:, bass.ds(GROUP * u, GROUP)], xl[:, bass.ds(GROUP * u, GROUP)])
                    MM(bank[:, f, :], w1_h[:, E, f, :], xs[0], start=True, stop=False)
                    MM(bank[:, f, :], w1_h[:, E, f, :], xs[1], start=False, stop=False)
                    MM(bank[:, f, :], w1_l[:, E, f, :], xs[0], start=False, stop=True).then_inc(s_sh_up, 1)

            def down(k, c, i):
                u = 2 * k + c
                pe.wait_ge(s_sh_low, 2 * (u + 1))
                if i is None or i >= 2:
                    pe.wait_ge(s_sh_acc, u - 1)
                MM(bank[:, 4 + c, :], b2_ones[:, :], b2_rows[:, :].unsqueeze(1).to_broadcast([P, TPG, D]),
                   start=True, stop=False, skip_group_check=True)
                for t in range(TPG):
                    for f in range(FC):
                        ps = bank[:, 4 + c, t * D:(t + 1) * D]
                        high, low = (parts[c][:, w, f, t * P:(t + 1) * P] for w in range(2))
                        MM(ps, high, w2_h[:, E, f, :], start=False, stop=False, skip_group_check=True)
                        MM(ps, high, w2_l[:, E, f, :], start=False, stop=False, skip_group_check=True)
                        last = MM(ps, low, w2_h[:, E, f, :], start=False, stop=(f == FC - 1), skip_group_check=True)
                last.then_inc(s_sh_down, 1)

            def body(k, c, i):
                at(scores, k, c, i, 0, range(2, 3))
                at(transpose_first, k, c, i, 1)
                at(transpose_second, k, c, i, -2)
                at(scores, k, c, i, 1, range(0, 1))
                at(router, k, c, i, -2)
                at(transpose_prob, k, c, i, 0)
                at(scores, k, c, i, 1, range(1, 2))
                at(ranks, k, c, i, -2)
                at(attend, k, c, i, 0)
                if i == GROUPS:
                    pe.wait_ge(s_picked, RELATIONS * GROUPS)
                    pe.wait_ge(s_axT, RELATIONS * GROUPS)
                    pe.wait_ge(s_w1l, 3)
                    up(0, 0, 0)

            pe.wait_ge(s_setup, 2)
            pe.wait_ge(s_const, 16 * CONST_DMAS)
            pipeline(pe, body, GROUPS, 2, 3)

            pe.wait_ge(s_count, GROUPS)
            pe.wait_ge(s_pos, GROUPS)
            MM(total_ps, ones[:, :], count[:, GROUPS % 2, :], start=True, stop=True).then_inc(s_total_ps, 1)
            up(0, 1, 1)
            pe.wait_ge(s_w2l, 1)
            down(0, 0, 0)
            pe.wait_ge(s_tab, 11)
            for f in range(FC):
                MM(bank[:, 6, f * RTILES:(f + 1) * RTILES], b1_rows[:, f * P:(f + 1) * P], is_expert[:, :], start=True, stop=True)
            MM(bank[:, 6, FC * RTILES:(FC + 1) * RTILES], b2_in[:, :], is_expert[:, :], start=True, stop=True).then_inc(s_bias, 1)
            with pe.Fori(1, HALF) as k:
                up(k, 0, None)
                down(k - 1, 1, None)
                up(k, 1, None)
                down(k, 0, None)
            down(HALF - 1, 1, None)
            pe.wait_ge(s_sh_acc, 2 * HALF)

            def body(k, c, i):
                t = 2 * k + c
                o = 1 - c
                e, e_last = (pe.snap(expert_of[b], min_val=0, max_val=E) for b in (c, o))
                if has(i, 1, RTILES):
                    pe.wait_ge(s_xt[o], 16 * (k + c + 1))
                    for h in range(RH):
                        last = nc.tensor.transpose(bank[:, 6 + o, h * P:(h + 1) * P], xt[:, o, h, 0:D], ident)
                    last.then_inc(s_xtT_ps, 1)
                if has(i, 0, RTILES):
                    pe.wait_ge(s_xtl, t + 1)
                for f in range(FC):
                    if has(i, 0, RTILES):
                        ps = bank[:, 2 * c + f // 2, RB * (f % 2):RB * (f % 2 + 1)]
                        wh = w1_h[:, bass.ds(e, 1), f, :].rearrange("p a f -> p (a f)")
                        wl = w1_l[:, bass.ds(e, 1), f, :].rearrange("p a f -> p (a f)")
                        MM(ps, wh, xth[:, c, :], start=True, stop=False)
                        MM(ps, wh, xtl[:, c, :], start=False, stop=False)
                        last = MM(ps, wl, xth[:, c, :], start=False, stop=True)
                        if f % 2:
                            last.then_inc(s_up, 1)
                    if f == 2 and has(i, 0, RTILES) and has(i, 1, RTILES):
                        e_next = expert(pe, t + 1, i)
                    if f == 2 and has(i, -2, RTILES):
                        pe.wait_ge(s_yT, t - 1)
                        for h in range(RH):
                            last = nc.tensor.transpose(bank[:, 4 + c, RB + h * P:RB + (h + 1) * P], yT[:, c, h * P:(h + 1) * P], ident)
                        last.then_inc(s_back, 1)
                if has(i, -1, RTILES):
                    if i is None or i >= 3:
                        pe.wait_ge(s_yt, t - 2)
                    hold(pe, s_low, 2 * t)
                    for f in range(FC):
                        ps = bank[:, 4 + o, 0:RB]
                        high, low = (parts[o][:, w, f, 0:RB] for w in range(2))
                        wh, wl = (w[:, bass.ds(e_last, 1), f, :].rearrange("p a d -> p (a d)") for w in (w2_h, w2_l))
                        MM(ps, wh, high, start=(f == 0), stop=False)
                        MM(ps, wh, low, start=False, stop=False)
                        last = MM(ps, wl, high, start=False, stop=(f == FC - 1))
                    last.then_inc(s_down, 1)
                if has(i, 0, RTILES) and has(i, 1, RTILES):
                    pe.reg_mov(expert_of[o], e_next)

            pe.wait_ge(s_w2l, 3)
            pe.wait_ge(s_table, 1)
            expert_of = [pe.alloc_register(f"expert_of_{c}") for c in range(2)]
            for c in range(2):
                pe.reg_mov(expert_of[c], expert(pe, 0, 0))
            pipeline(pe, body, RTILES, 1, 2, 3)

            pe.wait_ge(s_hid, 2 * RTILES)
            up(HALF, 0, None)
            up(HALF, 1, None)
            pe.wait_ge(s_yt, RTILES)
            down(HALF, 0, None)
            with pe.Fori(HALF + 1, 2 * HALF) as k:
                up(k, 0, None)
                down(k - 1, 1, None)
                up(k, 1, None)
                down(k, 0, None)
            down(2 * HALF - 1, 1, None)


def kernel(**inputs):
    import numpy as np
    from concourse import bacc
    from concourse.bass_utils import run_bass_kernel_spmd

    g = {name.replace("L0_gnn_", "").replace("L0_ffn_", ""): np.asarray(a) for name, a in inputs.items()}
    p = np.arange(P)
    constants = np.zeros((P, C_ALL), np.float32)
    constants[:, C_IDENT:C_IDENT + P] = np.eye(P)
    constants[:, C_TRI:C_TRI + P] = p[:, None] < p[None, :]
    constants[:, C_IOTA:C_IOTA + E] = np.arange(E)
    constants[:, C_REGION:C_REGION + E] = np.arange(E) * REGION
    constants[:, C_PART:C_PART + 3] = np.eye(P)[:, 0:3]
    constants[:, C_REL:C_REL + RELATIONS] = np.arange(1, RELATIONS + 1)
    constants[:, C_TILE:C_TILE + RTILES] = np.arange(RTILES)
    constants[:, C_ROW] = p
    places = np.zeros((P, K_ALL), np.int32)
    t, k = np.meshgrid(np.arange(-2 * TPG, 0), np.arange(TOP), indexing="ij")
    places[:, K_PLACE:K_PLACE + 2 * TPG * TOP] = p[:, None] + (t * P + k * TOKENS).reshape(1, -1)
    places[:, K_PAD:K_PAD + E * RH] = TOP * TOKENS + p[:, None] + P * np.arange(E * RH)
    places[:, K_SPARE:K_SPARE + E * RH] = TOP * TOKENS + E * RB + p[:, None] + P * np.arange(E * RH)

    def chunks(b):
        return np.ascontiguousarray(b.reshape(-1, P).T)

    arrays = {
        "x": g["x"].reshape(TOKENS, D),
        "adj": g["adj"].reshape(TOKENS, NODES),
        "a_relT": np.ascontiguousarray(g["a_rel"].T),
        "t_relT": np.ascontiguousarray(g["t_rel"].T),
        "time_w": g["time_w"].reshape(TIMES, 1),
        "wr": g["Wr"],
        "w1": np.concatenate([g["W1p"], g["W1s"][None]]),
        "w2": np.concatenate([g["W2p"], g["W2s"][None]]),
        "b1": np.concatenate([g["b1p"], g["b1s"][None]]),
        "b1T": chunks(np.concatenate([g["b1p"].reshape(-1), g["b1s"]])),
        "b2": np.concatenate([g["b2p"], g["b2s"][None]]),
        "b2s": np.ascontiguousarray(np.broadcast_to(g["b2s"], (P, D))),
        "constants": constants,
        "places": places,
    }
    nc = bacc.Bacc("TRN2", target_bir_lowering=False, num_devices=1)
    args = [nc.dram_tensor(n, a.shape, mybir.dt.from_np(a.dtype), kind="ExternalInput").ap() for n, a in arrays.items()]
    out = nc.dram_tensor("out", (TOKENS, D), F32, kind="ExternalOutput").ap()
    rows = nc.dram_tensor("expert_rows", (ROWS, RW), F32, kind="Internal").ap()
    results = nc.dram_tensor("expert_results", (YROWS, D), F32, kind="Internal").ap()
    build(nc, *args, out, rows, results)
    r = run_bass_kernel_spmd(nc, [arrays], core_ids=[0])
    return r.results[0]["out"].reshape(GRAPHS, NODES, D)
```
